# Optimizing a Trainium2 kernel written in Bass

```python
import numpy as np
import jax
import jax.numpy as jnp

def _softmax(x, axis=-1):
    return jax.nn.softmax(x, axis=axis)

def _gelu(x):
    return jax.nn.gelu(x, approximate=True)

def _silu(x):
    return jax.nn.silu(x)

def _sigmoid(x):
    return jax.nn.sigmoid(x)

def _layernorm(x, axis=-1, eps=1e-05):
    m = jnp.mean(x, axis=axis, keepdims=True)
    v = jnp.var(x, axis=axis, keepdims=True)
    return (x - m) / jnp.sqrt(v + eps)

def _scatter_add(tgt, idx, src, axis=0):
    return tgt.at[idx].add(src)

def _segment_sum(src, seg, n):
    return jax.ops.segment_sum(src, seg, n)
kernel_name = 'mk_xattn_seq_d4_seqx_r4_5b8101'

def setup_inputs(seed: int=0):
    np.random.seed(seed)
    _w = jnp.asarray

    def _rec_inputs():
        import jax
        import jax.numpy as jnp
        _rk = jax.random.key(seed)
        x = -0.0002928 + 1 * jax.random.normal(jax.random.fold_in(_rk, 1), (32, 128, 256), jnp.float32)
        _lenS = 128 - jax.random.randint(jax.random.fold_in(_rk, 7), (32,), 0, max(1, 128 // 4) + 1, jnp.int32)
        _lenS2 = 128 - jax.random.randint(jax.random.fold_in(_rk, 8), (32,), 0, max(1, 128 // 4) + 1, jnp.int32)
        _ctx_1024P = jax.random.normal(jax.random.fold_in(_rk, 11), (32, 16, 256), jnp.float32)
        _ctx_1024c = jax.random.dirichlet(jax.random.fold_in(_rk, 511), 0.3 * jnp.ones((16,), jnp.float32), (32, 128))
        _ctx_1024t = jnp.einsum('bsk,bkd->bsd', _ctx_1024c, _ctx_1024P)
        _ctx_1024t = _ctx_1024t * jax.lax.rsqrt(jnp.mean(jnp.square(_ctx_1024t)) + 1e-12) * 0.953939
        ctx_1024 = -1.39393e-06 + 0.999914 * (_ctx_1024t + 0.3 * jax.random.normal(jax.random.fold_in(_rk, 611), (32, 128, 256), jnp.float32))
        _validS = jnp.arange(128)[None, :] < _lenS[:, None]
        _validS2 = jnp.arange(128)[None, :] < _lenS2[:, None]
        _causal = jnp.tril(jnp.ones((128, 128), dtype=bool))
        mask_SxS2_ik0 = jnp.where(jnp.broadcast_to(_validS2[0:1, :], (128, 128)), 0, 1).astype(jnp.int32)
        mask_Bx1x1xS2_if1 = jnp.where(jnp.ones((32, 1, 1, 128), dtype=bool), 1, 0).astype(jnp.int32)
        return (x, ctx_1024, mask_SxS2_ik0, mask_Bx1x1xS2_if1)
    x, ctx_1024, mask_SxS2_ik0, mask_Bx1x1xS2_if1 = _rec_inputs()

    def _L0_xattn_setup():
        import jax, jax.numpy as jnp
        import numpy as np
        EPS = 1e-05

        def _layernorm(x, g, b):
            m = jnp.mean(x, axis=-1, keepdims=True)
            v = jnp.mean((x - m) ** 2, axis=-1, keepdims=True)
            return (x - m) / jnp.sqrt(v + EPS) * g + b

        def _mha(x, kv, Wq, Wk, Wv, mask, causal):
            m = mask[:, None]
            Q = jnp.einsum('bsd,hdk->bhsk', x, Wq) * m
            K = jnp.einsum('bsd,hdk->bhsk', kv, Wk) * m
            V = jnp.einsum('bsd,hdk->bhsk', kv, Wv) * m
            energy = jnp.einsum('bhsk,bhtk->bhst', Q, K)
            S = energy.shape[-1]
            lengths = jnp.sum(energy[:, :, 0, :] != 0, axis=-1)
            cols = jnp.arange(S)
            energy = jnp.where(cols[None, None, None, :] >= lengths[:, :, None, None], -jnp.inf, energy)
            if causal:
                energy = jnp.where(cols[None, :] > cols[:, None], -jnp.inf, energy)
            dk = Wq.shape[-1]
            score = jax.nn.softmax(energy / jnp.sqrt(jnp.asarray(dk, energy.dtype)), axis=-1)
            out = jnp.einsum('bhst,bhtk->bhsk', score, V) * m
            B, H, Sx, dkk = out.shape
            return out.transpose(0, 2, 1, 3).reshape(B, Sx, H * dkk)
        key = jax.random.key(seed)
        ks = jax.random.split(key, 20)
        B, S, D, H = (2, 512, 256, 16)
        dk = D // H
        sd = 0.02
        inp = {'x': jax.random.normal(ks[0], (B, S, D), jnp.float32), 'context': jax.random.normal(ks[1], (B, S, D), jnp.float32), 'Wq1': jax.random.normal(ks[2], (H, D, dk), jnp.float32) * sd, 'Wk1': jax.random.normal(ks[3], (H, D, dk), jnp.float32) * sd, 'Wv1': jax.random.normal(ks[4], (H, D, dk), jnp.float32) * sd, 'Wq2': jax.random.normal(ks[5], (H, D, dk), jnp.float32) * sd, 'Wk2': jax.random.normal(ks[6], (H, D, dk), jnp.float32) * sd, 'Wv2': jax.random.normal(ks[7], (H, D, dk), jnp.float32) * sd, 'ln1_g': jnp.ones((D,), jnp.float32), 'ln1_b': jnp.zeros((D,), jnp.float32), 'ln2_g': jnp.ones((D,), jnp.float32), 'ln2_b': jnp.zeros((D,), jnp.float32), 'ln3_g': jnp.ones((D,), jnp.float32), 'ln3_b': jnp.zeros((D,), jnp.float32), 'fc1_w': jax.random.normal(ks[8], (D, D), jnp.float32) * sd, 'fc1_b': jnp.zeros((D,), jnp.float32), 'fc2_w': jax.random.normal(ks[9], (D, D), jnp.float32) * sd, 'fc2_b': jnp.zeros((D,), jnp.float32)}
        return inp
    _L0_xattn_all = _L0_xattn_setup()
    _L0_xattn_in = {k: v for k, v in _L0_xattn_all.items() if k in ('Wq1', 'Wk1', 'Wv1', 'Wq2', 'Wk2', 'Wv2', 'ln1_g', 'ln1_b', 'ln2_g', 'ln2_b', 'ln3_g', 'ln3_b', 'fc1_w', 'fc1_b', 'fc2_w', 'fc2_b')}
    del _L0_xattn_all

    def _L1_xattn_setup():
        import jax, jax.numpy as jnp
        import numpy as np
        import math
        B, LT, LS, D, H, DFF = (2, 512, 512, 256, 16, 1024)
        DK = D // H

        def layer_norm(x, g, b, eps=1e-05):
            mu = jnp.mean(x, axis=-1, keepdims=True)
            var = jnp.var(x, axis=-1, keepdims=True)
            return (x - mu) * jax.lax.rsqrt(var + eps) * g + b

        def mha(q_in, k_in, v_in, wq, bq, wk, bk, wv, bv, wo, bo, mask):
            Bq, Lq, _ = q_in.shape
            Lk = k_in.shape[1]
            Q = (q_in @ wq + bq).reshape(Bq, Lq, H, DK).transpose(0, 2, 1, 3)
            K = (k_in @ wk + bk).reshape(Bq, Lk, H, DK).transpose(0, 2, 1, 3)
            V = (v_in @ wv + bv).reshape(Bq, Lk, H, DK).transpose(0, 2, 1, 3)
            scores = jnp.einsum('bhqd,bhkd->bhqk', Q, K) / math.sqrt(DK)
            if mask is not None:
                scores = jnp.where(mask == 0, jnp.float32(-1000000000.0), scores)
            attn = jax.nn.softmax(scores, axis=-1)
            out = jnp.einsum('bhqk,bhkd->bhqd', attn, V)
            out = out.transpose(0, 2, 1, 3).reshape(Bq, Lq, D)
            return out @ wo + bo
        key = jax.random.key(seed)
        ks = jax.random.split(key, 24)
        s = 0.02
        inp = {'x': jax.random.normal(ks[0], (B, LT, D), jnp.float32), 'encoder_output': jax.random.normal(ks[1], (B, LS, D), jnp.float32), 'tgt_mask': jnp.tril(jnp.ones((LT, LT), jnp.int32)), 'src_mask': jnp.ones((B, 1, 1, LS), jnp.int32)}
        names = ['self_wq', 'self_wk', 'self_wv', 'self_wo', 'cross_wq', 'cross_wk', 'cross_wv', 'cross_wo']
        for i, n in enumerate(names):
            inp[n] = jax.random.normal(ks[2 + i], (D, D), jnp.float32) * s
            inp[n.replace('w', 'b')] = jnp.zeros((D,), jnp.float32)
        inp['ff_w1'] = jax.random.normal(ks[10], (D, DFF), jnp.float32) * s
        inp['ff_b1'] = jnp.zeros((DFF,), jnp.float32)
        inp['ff_w2'] = jax.random.normal(ks[11], (DFF, D), jnp.float32) * s
        inp['ff_b2'] = jnp.zeros((D,), jnp.float32)
        for i, n in enumerate(['n1', 'n2', 'n3']):
            inp[n + '_g'] = jnp.ones((D,), jnp.float32)
            inp[n + '_b'] = jnp.zeros((D,), jnp.float32)
        return inp
    _L1_xattn_all = _L1_xattn_setup()
    _L1_xattn_in = {k: v for k, v in _L1_xattn_all.items() if k in ('self_wq', 'self_bq', 'self_wk', 'self_bk', 'self_wv', 'self_bv', 'self_wo', 'self_bo', 'cross_wq', 'cross_bq', 'cross_wk', 'cross_bk', 'cross_wv', 'cross_bv', 'cross_wo', 'cross_bo', 'ff_w1', 'ff_b1', 'ff_w2', 'ff_b2', 'n1_g', 'n1_b', 'n2_g', 'n2_b', 'n3_g', 'n3_b')}
    del _L1_xattn_all

    def _L2_xattn_setup():
        import jax, jax.numpy as jnp
        import numpy as np
        B, L, D_E = (2, 512, 256)
        H, D_Q = (16, 64)
        EPS = 1e-05
        key = jax.random.key(seed)
        ks = jax.random.split(key, 12)
        s_in = 1.0 / np.sqrt(D_E)
        s_mid = 1.0 / np.sqrt(H * D_Q)
        return {'pre_q': jax.random.normal(ks[0], (B, L, D_E), jnp.float32), 'pre_k': jax.random.normal(ks[1], (B, L, D_E), jnp.float32), 'Wq': jax.random.normal(ks[2], (D_E, H * D_Q), jnp.float32) * s_in, 'bq': jnp.zeros((H * D_Q,), jnp.float32), 'Wk': jax.random.normal(ks[3], (D_E, H * D_Q), jnp.float32) * s_in, 'bk': jnp.zeros((H * D_Q,), jnp.float32), 'Wv': jax.random.normal(ks[4], (D_E, H * D_Q), jnp.float32) * s_in, 'bv': jnp.zeros((H * D_Q,), jnp.float32), 'Wo': jax.random.normal(ks[5], (H * D_Q, D_E), jnp.float32) * s_mid, 'bo': jnp.zeros((D_E,), jnp.float32), 'gamma': jnp.ones((D_E,), jnp.float32), 'beta': jnp.zeros((D_E,), jnp.float32)}
    _L2_xattn_all = _L2_xattn_setup()
    _L2_xattn_in = {k: v for k, v in _L2_xattn_all.items() if k in ('Wq', 'bq', 'Wk', 'bk', 'Wv', 'bv', 'Wo', 'bo', 'gamma', 'beta')}
    del _L2_xattn_all

    def _L3_xattn_setup():
        import jax, jax.numpy as jnp
        import numpy as np
        D_MODEL = 256
        N_HEADS = 16
        D_K = D_MODEL // N_HEADS
        LN_EPS = 1e-05

        def _attention(query, key_value, W_qkv, b_qkv, W_o, b_o, ln_gamma, ln_beta):
            B, Sq, _ = query.shape
            Skv = key_value.shape[1]
            Wq, Wk, Wv = (W_qkv[:D_MODEL], W_qkv[D_MODEL:2 * D_MODEL], W_qkv[2 * D_MODEL:])
            bq, bk, bv = (b_qkv[:D_MODEL], b_qkv[D_MODEL:2 * D_MODEL], b_qkv[2 * D_MODEL:])
            Q = (query @ Wq.T + bq).reshape(B, Sq, N_HEADS, D_K).transpose(0, 2, 1, 3)
            K = (key_value @ Wk.T + bk).reshape(B, Skv, N_HEADS, D_K).transpose(0, 2, 1, 3)
            V = (key_value @ Wv.T + bv).reshape(B, Skv, N_HEADS, D_K).transpose(0, 2, 1, 3)
            scores = jnp.einsum('bhqd,bhkd->bhqk', Q.astype(jnp.float32), K.astype(jnp.float32))
            scores = scores / np.sqrt(D_K)
            attn = jax.nn.softmax(scores, axis=-1)
            context = jnp.einsum('bhqk,bhkd->bhqd', attn, V.astype(jnp.float32)).astype(query.dtype)
            context = context.transpose(0, 2, 1, 3).reshape(B, Sq, D_MODEL)
            output = context @ W_o.T + b_o
            x = output + query
            mu = jnp.mean(x, axis=-1, keepdims=True)
            var = jnp.mean(jnp.square(x - mu), axis=-1, keepdims=True)
            return (x - mu) / jnp.sqrt(var + LN_EPS) * ln_gamma + ln_beta
        key = jax.random.key(seed)
        ks = jax.random.split(key, 8)
        B, Sq, Skv = (2, 512, 512)
        scale = 1.0 / np.sqrt(D_MODEL)
        return {'query': jax.random.normal(ks[0], (B, Sq, D_MODEL), dtype=jnp.float32), 'key_value': jax.random.normal(ks[1], (B, Skv, D_MODEL), dtype=jnp.float32), 'W_qkv': jax.random.normal(ks[2], (3 * D_MODEL, D_MODEL), dtype=jnp.float32) * scale, 'b_qkv': jax.random.normal(ks[3], (3 * D_MODEL,), dtype=jnp.float32) * 0.01, 'W_o': jax.random.normal(ks[4], (D_MODEL, D_MODEL), dtype=jnp.float32) * scale, 'b_o': jax.random.normal(ks[5], (D_MODEL,), dtype=jnp.float32) * 0.01, 'ln_gamma': jnp.ones((D_MODEL,), dtype=jnp.float32), 'ln_beta': jnp.zeros((D_MODEL,), dtype=jnp.float32)}
    _L3_xattn_all = _L3_xattn_setup()
    _L3_xattn_in = {k: v for k, v in _L3_xattn_all.items() if k in ('W_qkv', 'b_qkv', 'W_o', 'b_o', 'ln_gamma', 'ln_beta')}
    del _L3_xattn_all
    return {'x': x, 'ctx_1024': ctx_1024, 'mask_SxS2_ik0': mask_SxS2_ik0, 'mask_Bx1x1xS2_if1': mask_Bx1x1xS2_if1, 'L0_xattn_Wq1': _L0_xattn_in['Wq1'], 'L0_xattn_Wk1': _L0_xattn_in['Wk1'], 'L0_xattn_Wv1': _L0_xattn_in['Wv1'], 'L0_xattn_Wq2': _L0_xattn_in['Wq2'], 'L0_xattn_Wk2': _L0_xattn_in['Wk2'], 'L0_xattn_Wv2': _L0_xattn_in['Wv2'], 'L0_xattn_ln1_g': _L0_xattn_in['ln1_g'], 'L0_xattn_ln1_b': _L0_xattn_in['ln1_b'], 'L0_xattn_ln2_g': _L0_xattn_in['ln2_g'], 'L0_xattn_ln2_b': _L0_xattn_in['ln2_b'], 'L0_xattn_ln3_g': _L0_xattn_in['ln3_g'], 'L0_xattn_ln3_b': _L0_xattn_in['ln3_b'], 'L0_xattn_fc1_w': _L0_xattn_in['fc1_w'], 'L0_xattn_fc1_b': _L0_xattn_in['fc1_b'], 'L0_xattn_fc2_w': _L0_xattn_in['fc2_w'], 'L0_xattn_fc2_b': _L0_xattn_in['fc2_b'], 'L1_xattn_self_wq': _L1_xattn_in['self_wq'], 'L1_xattn_self_bq': _L1_xattn_in['self_bq'], 'L1_xattn_self_wk': _L1_xattn_in['self_wk'], 'L1_xattn_self_bk': _L1_xattn_in['self_bk'], 'L1_xattn_self_wv': _L1_xattn_in['self_wv'], 'L1_xattn_self_bv': _L1_xattn_in['self_bv'], 'L1_xattn_self_wo': _L1_xattn_in['self_wo'], 'L1_xattn_self_bo': _L1_xattn_in['self_bo'], 'L1_xattn_cross_wq': _L1_xattn_in['cross_wq'], 'L1_xattn_cross_bq': _L1_xattn_in['cross_bq'], 'L1_xattn_cross_wk': _L1_xattn_in['cross_wk'], 'L1_xattn_cross_bk': _L1_xattn_in['cross_bk'], 'L1_xattn_cross_wv': _L1_xattn_in['cross_wv'], 'L1_xattn_cross_bv': _L1_xattn_in['cross_bv'], 'L1_xattn_cross_wo': _L1_xattn_in['cross_wo'], 'L1_xattn_cross_bo': _L1_xattn_in['cross_bo'], 'L1_xattn_ff_w1': _L1_xattn_in['ff_w1'], 'L1_xattn_ff_b1': _L1_xattn_in['ff_b1'], 'L1_xattn_ff_w2': _L1_xattn_in['ff_w2'], 'L1_xattn_ff_b2': _L1_xattn_in['ff_b2'], 'L1_xattn_n1_g': _L1_xattn_in['n1_g'], 'L1_xattn_n1_b': _L1_xattn_in['n1_b'], 'L1_xattn_n2_g': _L1_xattn_in['n2_g'], 'L1_xattn_n2_b': _L1_xattn_in['n2_b'], 'L1_xattn_n3_g': _L1_xattn_in['n3_g'], 'L1_xattn_n3_b': _L1_xattn_in['n3_b'], 'L2_xattn_Wq': _L2_xattn_in['Wq'], 'L2_xattn_bq': _L2_xattn_in['bq'], 'L2_xattn_Wk': _L2_xattn_in['Wk'], 'L2_xattn_bk': _L2_xattn_in['bk'], 'L2_xattn_Wv': _L2_xattn_in['Wv'], 'L2_xattn_bv': _L2_xattn_in['bv'], 'L2_xattn_Wo': _L2_xattn_in['Wo'], 'L2_xattn_bo': _L2_xattn_in['bo'], 'L2_xattn_gamma': _L2_xattn_in['gamma'], 'L2_xattn_beta': _L2_xattn_in['beta'], 'L3_xattn_W_qkv': _L3_xattn_in['W_qkv'], 'L3_xattn_b_qkv': _L3_xattn_in['b_qkv'], 'L3_xattn_W_o': _L3_xattn_in['W_o'], 'L3_xattn_b_o': _L3_xattn_in['b_o'], 'L3_xattn_ln_gamma': _L3_xattn_in['ln_gamma'], 'L3_xattn_ln_beta': _L3_xattn_in['ln_beta']}

def reference(x, ctx_1024, mask_SxS2_ik0, mask_Bx1x1xS2_if1, L0_xattn_Wq1, L0_xattn_Wk1, L0_xattn_Wv1, L0_xattn_Wq2, L0_xattn_Wk2, L0_xattn_Wv2, L0_xattn_ln1_g, L0_xattn_ln1_b, L0_xattn_ln2_g, L0_xattn_ln2_b, L0_xattn_ln3_g, L0_xattn_ln3_b, L0_xattn_fc1_w, L0_xattn_fc1_b, L0_xattn_fc2_w, L0_xattn_fc2_b, L1_xattn_self_wq, L1_xattn_self_bq, L1_xattn_self_wk, L1_xattn_self_bk, L1_xattn_self_wv, L1_xattn_self_bv, L1_xattn_self_wo, L1_xattn_self_bo, L1_xattn_cross_wq, L1_xattn_cross_bq, L1_xattn_cross_wk, L1_xattn_cross_bk, L1_xattn_cross_wv, L1_xattn_cross_bv, L1_xattn_cross_wo, L1_xattn_cross_bo, L1_xattn_ff_w1, L1_xattn_ff_b1, L1_xattn_ff_w2, L1_xattn_ff_b2, L1_xattn_n1_g, L1_xattn_n1_b, L1_xattn_n2_g, L1_xattn_n2_b, L1_xattn_n3_g, L1_xattn_n3_b, L2_xattn_Wq, L2_xattn_bq, L2_xattn_Wk, L2_xattn_bk, L2_xattn_Wv, L2_xattn_bv, L2_xattn_Wo, L2_xattn_bo, L2_xattn_gamma, L2_xattn_beta, L3_xattn_W_qkv, L3_xattn_b_qkv, L3_xattn_W_o, L3_xattn_b_o, L3_xattn_ln_gamma, L3_xattn_ln_beta):
    import jax
    import jax.numpy as jnp

    def _L0_xattn_ref(x, context, Wq1, Wk1, Wv1, Wq2, Wk2, Wv2, ln1_g, ln1_b, ln2_g, ln2_b, ln3_g, ln3_b, fc1_w, fc1_b, fc2_w, fc2_b):
        import jax, jax.numpy as jnp
        import numpy as np
        EPS = 1e-05

        def _layernorm(x, g, b):
            m = jnp.mean(x, axis=-1, keepdims=True)
            v = jnp.mean((x - m) ** 2, axis=-1, keepdims=True)
            return (x - m) / jnp.sqrt(v + EPS) * g + b

        def _mha(x, kv, Wq, Wk, Wv, mask, causal):
            m = mask[:, None]
            Q = jnp.einsum('bsd,hdk->bhsk', x, Wq) * m
            K = jnp.einsum('bsd,hdk->bhsk', kv, Wk) * m
            V = jnp.einsum('bsd,hdk->bhsk', kv, Wv) * m
            energy = jnp.einsum('bhsk,bhtk->bhst', Q, K)
            S = energy.shape[-1]
            lengths = jnp.sum(energy[:, :, 0, :] != 0, axis=-1)
            cols = jnp.arange(S)
            energy = jnp.where(cols[None, None, None, :] >= lengths[:, :, None, None], -jnp.inf, energy)
            if causal:
                energy = jnp.where(cols[None, :] > cols[:, None], -jnp.inf, energy)
            dk = Wq.shape[-1]
            score = jax.nn.softmax(energy / jnp.sqrt(jnp.asarray(dk, energy.dtype)), axis=-1)
            out = jnp.einsum('bhst,bhtk->bhsk', score, V) * m
            B, H, Sx, dkk = out.shape
            return out.transpose(0, 2, 1, 3).reshape(B, Sx, H * dkk)
        mask0 = 1.0 - jnp.all(x == 0, axis=2, keepdims=True).astype(x.dtype)
        z = _mha(x, x, Wq1, Wk1, Wv1, mask0, causal=True)
        x1 = _layernorm(x + z, ln1_g, ln1_b)
        mask1 = 1.0 - jnp.all(x1 == 0, axis=2, keepdims=True).astype(x1.dtype)
        z = _mha(x1, context, Wq2, Wk2, Wv2, mask1, causal=False)
        x2 = _layernorm(x1 + z, ln2_g, ln2_b)
        z = jnp.maximum(x2 @ fc1_w.T + fc1_b, 0.0) * mask0
        z = (z @ fc2_w.T + fc2_b) * mask0
        return _layernorm(x2 + z, ln3_g, ln3_b)

    def _L1_xattn_ref(x, encoder_output, tgt_mask, src_mask, self_wq, self_bq, self_wk, self_bk, self_wv, self_bv, self_wo, self_bo, cross_wq, cross_bq, cross_wk, cross_bk, cross_wv, cross_bv, cross_wo, cross_bo, ff_w1, ff_b1, ff_w2, ff_b2, n1_g, n1_b, n2_g, n2_b, n3_g, n3_b):
        import jax, jax.numpy as jnp
        import numpy as np
        import math
        B, LT, LS, D, H, DFF = (2, 512, 512, 256, 16, 1024)
        DK = D // H

        def layer_norm(x, g, b, eps=1e-05):
            mu = jnp.mean(x, axis=-1, keepdims=True)
            var = jnp.var(x, axis=-1, keepdims=True)
            return (x - mu) * jax.lax.rsqrt(var + eps) * g + b

        def mha(q_in, k_in, v_in, wq, bq, wk, bk, wv, bv, wo, bo, mask):
            Bq, Lq, _ = q_in.shape
            Lk = k_in.shape[1]
            Q = (q_in @ wq + bq).reshape(Bq, Lq, H, DK).transpose(0, 2, 1, 3)
            K = (k_in @ wk + bk).reshape(Bq, Lk, H, DK).transpose(0, 2, 1, 3)
            V = (v_in @ wv + bv).reshape(Bq, Lk, H, DK).transpose(0, 2, 1, 3)
            scores = jnp.einsum('bhqd,bhkd->bhqk', Q, K) / math.sqrt(DK)
            if mask is not None:
                scores = jnp.where(mask == 0, jnp.float32(-1000000000.0), scores)
            attn = jax.nn.softmax(scores, axis=-1)
            out = jnp.einsum('bhqk,bhkd->bhqd', attn, V)
            out = out.transpose(0, 2, 1, 3).reshape(Bq, Lq, D)
            return out @ wo + bo
        attn_out = mha(x, x, x, self_wq, self_bq, self_wk, self_bk, self_wv, self_bv, self_wo, self_bo, tgt_mask)
        x = layer_norm(x + attn_out, n1_g, n1_b)
        attn_out = mha(x, encoder_output, encoder_output, cross_wq, cross_bq, cross_wk, cross_bk, cross_wv, cross_bv, cross_wo, cross_bo, src_mask)
        x = layer_norm(x + attn_out, n2_g, n2_b)
        ff_out = jax.nn.gelu(x @ ff_w1 + ff_b1, approximate=False) @ ff_w2 + ff_b2
        x = layer_norm(x + ff_out, n3_g, n3_b)
        return x

    def _L2_xattn_ref(pre_q, pre_k, Wq, bq, Wk, bk, Wv, bv, Wo, bo, gamma, beta):
        import jax, jax.numpy as jnp
        import numpy as np
        B, L, D_E = (2, 512, 256)
        H, D_Q = (16, 64)
        EPS = 1e-05
        b, ql, _ = pre_q.shape
        kl = pre_k.shape[1]
        q = (pre_q @ Wq + bq).reshape(b, ql, H, D_Q)
        k = (pre_k @ Wk + bk).reshape(b, kl, H, D_Q)
        v = (pre_k @ Wv + bv).reshape(b, kl, H, D_Q)
        scores = jnp.einsum('bqhd,bkhd->bhqk', q, k) / jnp.sqrt(jnp.float32(D_Q))
        attn = jax.nn.softmax(scores, axis=-1)
        ctx = jnp.einsum('bhqk,bkhd->bqhd', attn, v).reshape(b, ql, H * D_Q)
        out = ctx @ Wo + bo
        x = pre_q + out
        mu = jnp.mean(x, axis=-1, keepdims=True)
        var = jnp.mean(jnp.square(x - mu), axis=-1, keepdims=True)
        return (x - mu) * jax.lax.rsqrt(var + EPS) * gamma + beta

    def _L3_xattn_ref(query, key_value, W_qkv, b_qkv, W_o, b_o, ln_gamma, ln_beta):
        import jax, jax.numpy as jnp
        import numpy as np
        D_MODEL = 256
        N_HEADS = 16
        D_K = D_MODEL // N_HEADS
        LN_EPS = 1e-05

        def _attention(query, key_value, W_qkv, b_qkv, W_o, b_o, ln_gamma, ln_beta):
            B, Sq, _ = query.shape
            Skv = key_value.shape[1]
            Wq, Wk, Wv = (W_qkv[:D_MODEL], W_qkv[D_MODEL:2 * D_MODEL], W_qkv[2 * D_MODEL:])
            bq, bk, bv = (b_qkv[:D_MODEL], b_qkv[D_MODEL:2 * D_MODEL], b_qkv[2 * D_MODEL:])
            Q = (query @ Wq.T + bq).reshape(B, Sq, N_HEADS, D_K).transpose(0, 2, 1, 3)
            K = (key_value @ Wk.T + bk).reshape(B, Skv, N_HEADS, D_K).transpose(0, 2, 1, 3)
            V = (key_value @ Wv.T + bv).reshape(B, Skv, N_HEADS, D_K).transpose(0, 2, 1, 3)
            scores = jnp.einsum('bhqd,bhkd->bhqk', Q.astype(jnp.float32), K.astype(jnp.float32))
            scores = scores / np.sqrt(D_K)
            attn = jax.nn.softmax(scores, axis=-1)
            context = jnp.einsum('bhqk,bhkd->bhqd', attn, V.astype(jnp.float32)).astype(query.dtype)
            context = context.transpose(0, 2, 1, 3).reshape(B, Sq, D_MODEL)
            output = context @ W_o.T + b_o
            x = output + query
            mu = jnp.mean(x, axis=-1, keepdims=True)
            var = jnp.mean(jnp.square(x - mu), axis=-1, keepdims=True)
            return (x - mu) / jnp.sqrt(var + LN_EPS) * ln_gamma + ln_beta
        return _attention(query, key_value, W_qkv, b_qkv, W_o, b_o, ln_gamma, ln_beta)
    x = _L0_xattn_ref(x, ctx_1024, L0_xattn_Wq1, L0_xattn_Wk1, L0_xattn_Wv1, L0_xattn_Wq2, L0_xattn_Wk2, L0_xattn_Wv2, L0_xattn_ln1_g, L0_xattn_ln1_b, L0_xattn_ln2_g, L0_xattn_ln2_b, L0_xattn_ln3_g, L0_xattn_ln3_b, L0_xattn_fc1_w, L0_xattn_fc1_b, L0_xattn_fc2_w, L0_xattn_fc2_b)
    x = _L1_xattn_ref(x, ctx_1024, mask_SxS2_ik0, mask_Bx1x1xS2_if1, L1_xattn_self_wq, L1_xattn_self_bq, L1_xattn_self_wk, L1_xattn_self_bk, L1_xattn_self_wv, L1_xattn_self_bv, L1_xattn_self_wo, L1_xattn_self_bo, L1_xattn_cross_wq, L1_xattn_cross_bq, L1_xattn_cross_wk, L1_xattn_cross_bk, L1_xattn_cross_wv, L1_xattn_cross_bv, L1_xattn_cross_wo, L1_xattn_cross_bo, L1_xattn_ff_w1, L1_xattn_ff_b1, L1_xattn_ff_w2, L1_xattn_ff_b2, L1_xattn_n1_g, L1_xattn_n1_b, L1_xattn_n2_g, L1_xattn_n2_b, L1_xattn_n3_g, L1_xattn_n3_b)
    x = _L2_xattn_ref(x, ctx_1024, L2_xattn_Wq, L2_xattn_bq, L2_xattn_Wk, L2_xattn_bk, L2_xattn_Wv, L2_xattn_bv, L2_xattn_Wo, L2_xattn_bo, L2_xattn_gamma, L2_xattn_beta)
    x = _L3_xattn_ref(x, ctx_1024, L3_xattn_W_qkv, L3_xattn_b_qkv, L3_xattn_W_o, L3_xattn_b_o, L3_xattn_ln_gamma, L3_xattn_ln_beta)
    return x

_drawn_inputs = setup_inputs


def setup_inputs(seed=0):
    import zlib

    import numpy as np

    out = dict(_drawn_inputs(seed))
    spreads = {'L0_xattn_ln1_g': (1.0, 0.2),
     'L0_xattn_ln1_b': (0.0, 0.1),
     'L0_xattn_ln2_g': (1.0, 0.2),
     'L0_xattn_ln2_b': (0.0, 0.1),
     'L0_xattn_ln3_g': (1.0, 0.2),
     'L0_xattn_ln3_b': (0.0, 0.1),
     'L0_xattn_fc1_b': (0.0, 0.54),
     'L0_xattn_fc2_b': (0.0, 0.1),
     'L1_xattn_self_bq': (0.0, 0.1),
     'L1_xattn_self_bk': (0.0, 0.1),
     'L1_xattn_self_bv': (0.0, 0.391),
     'L1_xattn_self_bo': (0.0, 0.1),
     'L1_xattn_cross_bq': (0.0, 0.8),
     'L1_xattn_cross_bk': (0.0, 0.8),
     'L1_xattn_cross_bv': (0.0, 0.318),
     'L1_xattn_cross_bo': (0.0, 0.1),
     'L1_xattn_ff_b1': (0.0, 0.296),
     'L1_xattn_ff_b2': (0.0, 0.1),
     'L1_xattn_n1_g': (1.0, 0.2),
     'L1_xattn_n1_b': (0.0, 0.1),
     'L1_xattn_n2_g': (1.0, 0.2),
     'L1_xattn_n2_b': (0.0, 0.1),
     'L1_xattn_n3_g': (1.0, 0.2),
     'L1_xattn_n3_b': (0.0, 0.1),
     'L2_xattn_bq': (0.0, 0.444),
     'L2_xattn_bk': (0.0, 0.8),
     'L2_xattn_bv': (0.0, 0.1),
     'L2_xattn_bo': (0.0, 0.1),
     'L2_xattn_gamma': (1.0, 0.2),
     'L2_xattn_beta': (0.0, 0.1),
     'L3_xattn_ln_gamma': (1.0, 0.2),
     'L3_xattn_ln_beta': (0.0, 0.1)}
    factors = {'L0_xattn_Wq1': 8.0,
     'L0_xattn_Wk1': 8.0,
     'L0_xattn_Wq2': 8.0,
     'L0_xattn_Wk2': 8.0,
     'L1_xattn_self_wv': 2.707,
     'L1_xattn_cross_wq': 8.0,
     'L1_xattn_cross_wk': 8.0,
     'L3_xattn_b_qkv': 6.507,
     'L3_xattn_b_o': 6.392}
    for name, (base, spread) in spreads.items():
        noise = np.random.default_rng([zlib.crc32(name.encode()), seed]).standard_normal(out[name].shape)
        drawn = base * np.exp(spread * noise) if base else spread * noise
        out[name] = jnp.asarray(drawn.astype(out[name].dtype))
    for name, factor in factors.items():
        out[name] = (out[name] * factor).astype(out[name].dtype)
    return out
```

```python
from contextlib import ExitStack

import numpy as np
import concourse.bass as bass
from concourse import mybir

ALU = mybir.AluOpType
ACT = mybir.ActivationFunctionType
AX_X = mybir.AxisListType.X
F32 = mybir.dt.float32
BF16 = mybir.dt.bfloat16
I32 = mybir.dt.int32

P = 128
BATCH, SEQ, D, HEADS = 32, 128, 256, 16
KC = D // P
DK, DK2 = 16, 64
FF0, FF1 = 256, 1024
STREAMS = 4
ROUNDS = BATCH // STREAMS
ATTS = 6
HU = HEADS // 2
UNITS = ATTS * STREAMS * 2
BIG = 2.0 ** 100
EPS = 1e-5
WIDE = 4
MASKED_BY_LENGTH = (0, 1)

WEIGHTS = [("q0", D), ("k0", D), ("v0", D), ("q1", D), ("k1", D), ("v1", D), ("f0", FF0), ("g0", D),
           ("q2", D), ("k2", D), ("v2", D), ("o2", D), ("q3", D), ("k3", D), ("v3", D), ("o3", D),
           ("f1", FF1), ("g1", D), ("q4", HEADS * DK2), ("k4", HEADS * DK2), ("v4", HEADS * DK2), ("o4", D),
           ("q5", D), ("k5", D), ("v5", D), ("o5", D)]
W_ROWS = {"g1": FF1, "o4": HEADS * DK2}
COLUMN_BIASES = [("f0", FF0), ("q2", D), ("k2", D), ("q3", D), ("k3", D), ("f1", FF1),
                 ("q4", HEADS * DK2), ("k4", HEADS * DK2), ("q5", D), ("k5", D)]
ROWS = [("ln0g", D), ("ln0b", D), ("ln1g", D), ("ln1b", D), ("lnfg", D), ("lnfb", D), ("g0", D),
        ("v2", D), ("o2", D), ("ln2g", D), ("ln2b", D), ("v3", D), ("o3", D), ("ln3g", D), ("ln3b", D),
        ("g1", D), ("lnhg", D), ("lnhb", D), ("v4", HEADS * DK2), ("o4", D), ("ln4g", D), ("ln4b", D),
        ("v5", D), ("o5", D), ("ln5g", D), ("ln5b", D)]
ROWS_EARLY = 7


def offsets(parts, width=lambda n: n):
    at, out = 0, {}
    for name, n in parts:
        out[name] = at
        at += width(n)
    return out, at


W_AT, W_COLS = {}, 0
for _name, _n in WEIGHTS:
    W_AT[_name] = W_COLS
    W_COLS += W_ROWS.get(_name, D) // P * _n
CB_AT, CB_COLS = offsets(COLUMN_BIASES, lambda n: n // P)
ROW_AT, ROW_COLS = offsets(ROWS)

CONSTS = [("ident", P), ("causal", P), ("khead", 4), ("qhead", HU), ("iota", P), ("hsel", HU * P)]
C_AT, C_COLS = offsets(CONSTS)

LN_OF = {("att", 0): "ln0", ("att", 1): "ln1", ("ff", 1): "lnf", ("att", 2): "ln2", ("att", 3): "ln3",
         ("ff", 3): "lnh", ("att", 4): "ln4", ("att", 5): "ln5"}
XT_AFTER = [None, ("att", 0), ("att", 1), ("ff", 1), ("att", 2), ("att", 3), ("ff", 3), ("att", 4)]
XT_FOR_ATT = [0, 1, 3, 4, 6, 7]


def make_order():
    extra = {}

    def put(step, slot, *item):
        extra.setdefault((step, slot), []).append(item)

    plan = {
        -1: [(4, 0, "XT", 0), (4, 0, "CT"), (5, 0, "K"), (5, 1, "Q"), (6, 0, "L", 0), (6, 2, "L", 1), (7, 0, "V")],
        0: [(3, 0, "E1"), (4, 0, "XT", 1), (4, 0, "CM"), (5, 0, "K"), (5, 1, "Q"), (6, 0, "L", 0), (6, 2, "L", 1),
            (7, 0, "V")],
        1: [(3, 0, "E1"), (4, 0, "XT", 2), (4, 2, "F1", 0), (5, 0, "F2"), (6, 0, "XT", 3), (6, 1, "K"), (6, 2, "Q"),
            (7, 0, "V")],
        2: [(3, 0, "E1"), (3, 1, "E2"), (3, 2, "E3"), (5, 0, "K"), (5, 1, "XT", 4), (6, 0, "Q"), (7, 0, "V")],
        3: [(3, 0, "E1"), (3, 1, "E2"), (3, 2, "E3"), (4, 1, "XT", 5), (4, 2, "F1", 0), (4, 2, "F1", 1), (5, 1, "F2"),
            (5, 2, "K", 0), (6, 0, "K", 1), (6, 1, "XT", 6), (6, 2, "Q", 0), (6, 2, "Q", 1), (7, 0, "V", 0),
            (7, 1, "V", 1)],
        4: [(3, 0, "E3"), (5, 0, "K"), (5, 1, "XT", 7), (6, 0, "Q"), (7, 0, "V")],
        5: [(3, 0, "E1"), (3, 1, "E2"), (3, 2, "E3")],
    }
    for s in range(STREAMS):
        for a, pieces in plan.items():
            for step, slot, kind, *c in pieces:
                b = a + (kind in ("K", "Q", "V", "L"))
                put(8 * a + 2 * s + step, slot, kind, *((s,) if kind in ("CT", "CM") else (c[0], s) if kind == "XT"
                    else (b, s, c[0] if c else 0)))
    out = []
    for n in range(-4, UNITS + 4):
        live = lambda m: 0 <= m < UNITS
        out += [("T", n - 1, 0), ("T", n - 1, 1)] * live(n - 1)
        out += extra.pop((n, 0), [])
        out += [("A", n)] * live(n)
        out += [("S", n + 1)] * live(n + 1)
        out += [("PV", n - 1, 0)] * live(n - 1)
        out += extra.pop((n, 1), [])
        out += [("PV", n - 1, 1)] * live(n - 1)
        out += extra.pop((n, 2), [])
    assert not extra, extra
    return out


ORDER = make_order()
BY_ACT = {"T", "XT", "CT", "CM", "Q", "E2", "F1"}
BY_DVE = {"K", "V", "L", "E1", "E3", "F2"}


def unit(n):
    return n // (2 * STREAMS), n // 2 % STREAMS, n % 2


def norms():
    out = []
    for it in ORDER:
        if it[0] == "E1" and it[1] in (0, 1) or it[0] == "E3":
            out.append(("att", it[1], it[2]))
        elif it[0] == "F2":
            out.append(("ff", it[1], it[2]))
    return out


def xb_pieces():
    after = {("ff", 1): "o2", ("att", 2): "o3", ("ff", 3): "o4", ("att", 4): "o5", ("att", 1): "g0", ("att", 3): "g1"}
    return [(after[n[:2]], n[2]) for n in norms() if n[:2] in after], after


INDEX = {
    "tile": [it for it in ORDER if it[0] in BY_ACT | BY_DVE],
    "tile_act": [it for it in ORDER if it[0] in BY_ACT],
    "tile_dve": [it for it in ORDER if it[0] in BY_DVE],
    "unit": [it[1] for it in ORDER if it[0] == "S"],
    "half": [it[1:] for it in ORDER if it[0] == "PV"],
    "ctx": [it[1] for it in ORDER if it[0] == "PV" and it[2] == 1 and (it[1] % 2 == 1 or unit(it[1])[0] == WIDE)],
    "e1": [it[1:] for it in ORDER if it[0] == "E1"],
    "residual": [it[1:3] for it in ORDER if it[0] == "E1" and it[1] in (0, 1)],
    "norm": norms(),
    "xb": xb_pieces()[0],
    "length": [it[1:] for it in ORDER if it[0] == "L"],
    "q0": [it[1:3] for it in ORDER if it[0] == "Q" and it[1] in MASKED_BY_LENGTH],
    "stream": list(range(STREAMS)),
    "wide": [n for n in range(UNITS) if unit(n)[0] == WIDE],
}
COUNT = {k: len(v) for k, v in INDEX.items()}
AT = {k: {key: i for i, key in enumerate(v)} for k, v in INDEX.items()}
XB_AFTER = xb_pieces()[1]


def build(nc, x, ctx_in, mask_ss, mask_bs, weights, col_bias, row_vec, consts, out):
    with ExitStack() as stack:
        def sb(name, shape, dt=F32):
            return stack.enter_context(nc.sbuf_tensor(name, shape, dt))

        def sem(name):
            return stack.enter_context(nc.semaphore(name))

        W = sb("W", [P, W_COLS])
        RV = sb("RV", [P, ROW_COLS])
        CB = sb("CB", [P, CB_COLS])
        ident = sb("ident", [P, P])
        ident_b = sb("ident_b", [P, P], BF16)
        causal_b = sb("causal_b", [P, P], BF16)
        khead = sb("khead", [P, 4])
        qhead = sb("qhead", [P, HU])
        iota = sb("iota", [HU, P])
        hsel_b = sb("hsel_b", [HU, HU * P], BF16)
        ones_b = sb("ones_b", [HU, P], BF16)
        half = sb("half", [P, 1])
        mask_ss_b = sb("mask_ss_b", [P, P], BF16)

        per_stream = lambda name, shape, dt=F32: [sb(f"{name}{s}", shape, dt) for s in range(STREAMS)]
        per_pair = lambda name, shape, dt=F32: [sb(f"{name}{i}", shape, dt) for i in range(2)]
        x_in, c_in = per_stream("x_in", [P, D]), per_stream("c_in", [P, D])
        X, XB = per_stream("X", [P, D]), per_stream("XB", [P, D])
        XT, CT = per_stream("XT", [P, D]), per_stream("CT", [P, D])
        seen0, seen1 = per_stream("seen0_", [P, 1]), per_stream("seen1_", [P, 1])
        mask_bs_i, mask_bs_b = per_stream("mask_bs_i", [1, P], I32), per_stream("mask_bs_b", [1, P], BF16)
        QT, KT = per_pair("QT", [P, 8 * P]), per_pair("KT", [P, 8 * P])
        V16, V64 = per_pair("V16_", [P, HEADS, 32]), per_pair("V64_", [P, HEADS * DK2])
        OT, O, OnT = per_pair("OT", [P, 8 * P]), per_pair("O", [P, D]), per_pair("OnT", [P, D])
        KTp, CmT = [v[:, 0:D] for v in V64], [v[:, D:2 * D] for v in V64]
        LB = [v[0:HU, 2 * D:2 * D + HU * P // 2].bitcast(BF16) for v in V64]
        q0 = per_pair("q0_", [P, 2, HU])
        rsum = per_pair("rsum", [P, HEADS])
        Pr = per_pair("Pr", [P, HU * P])
        PT = per_pair("PT", [P, 4 * P])
        nmax = per_pair("nmax", [P, HU])
        wsum, wrec = per_pair("wsum", [P, HU]), per_pair("wrec", [P, HU])
        stats, mv, rstd, xc = sb("stats", [P, 6]), sb("mv", [P, 2]), per_pair("rstd", [P, 1]), sb("xc", [P, D])
        ne, cnt, crec, lval, lrow = (sb("ne", [HU, P]), sb("cnt", [HU, 1]), sb("crec", [HU, 1]), sb("lval", [HU, 1]),
                                     sb("lrow", [HU, P], BF16))
        absmax = sb("absmax", [P, 1])

        ps = lambda name, n: stack.enter_context(nc.psum_tensor(name, [P, n], F32))
        SC = [ps("SC0", 1024), ps("SC1", 1024)]
        OTp = ps("OTp", 512)
        M = [ps(f"M{i}", 512) for i in range(3)]

        w_in = {name: sem(f"w_{name}") for name, _ in WEIGHTS}
        rows_in, rows_late_in, cols_in, consts_in, masks_in = (sem("rows_in"), sem("rows_late_in"), sem("cols_in"),
                                                               sem("consts_in"), sem("masks_in"))
        m_loaded, mask_done = [sem(f"m_loaded{s}") for s in range(STREAMS)], sem("mask_done")
        x_loaded, c_loaded, stored = ([sem(f"x_loaded{s}") for s in range(STREAMS)],
                                      [sem(f"c_loaded{s}") for s in range(STREAMS)],
                                      [sem(f"stored{s}") for s in range(STREAMS)])
        ready_dve, ready_act = sem("ready_dve"), sem("ready_act")
        cols_scaled = sem("cols_scaled")
        scores = sem("scores")
        context = sem("context")
        tile_full = sem("tile_full")
        tile_act = sem("tile_act")
        tile_dve = sem("tile_dve")
        probs = sem("probs")
        context_out = sem("context_out")
        maxima = sem("maxima")
        q0_done = sem("q0_done")
        len_cnt, len_rec, len_val, len_row, len_mask = (sem("len_cnt"), sem("len_rec"),
                                                                sem("len_val"), sem("len_row"), sem("len_mask"))
        recip_done, recip_masked = sem("recip_done"), sem("recip_masked")
        summed, stats_done, var_done, eps_done, centred, normed = (sem("summed"), sem("stats_done"), sem("var_done"),
                                                         sem("eps_done"), sem("centred"), sem("normed"))
        rstd_done, xb_half, xb_done = sem("rstd_done"), sem("xb_half"), sem("xb_done")
        abs0, seen0_done, abs1, seen1_done, cm_done = (sem("abs0"), sem("seen0_done"), sem("abs1"), sem("seen1_done"),
                                                       sem("cm_done"))
        wide_sum, wide_rec, wide_norm = sem("wide_sum"), sem("wide_rec"), sem("wide_norm")

        def weight(name, k, a, b):
            n = dict(WEIGHTS)[name]
            return W[:, W_AT[name] + k * n + a:W_AT[name] + k * n + b]

        def row(name, n=D, at=0):
            return RV[:, ROW_AT[name] + at:ROW_AT[name] + at + n]

        from_one = (tile_act, probs, context_out, tile_dve)

        def waiter(eng, r):
            def wait(s, kind, key):
                eng.wait_ge(s, r * COUNT[kind] + (AT[kind][key] + 1 + (s in from_one)))

            def wait_nth(s, kind, i):
                assert s in from_one
                eng.wait_ge(s, r * COUNT[kind] + (max(i + 1, 0) + 1))
            return wait, wait_nth

        def tile_of(it):
            return M[AT["tile"][it] % len(M)]

        def width(a):
            return DK2 if a == WIDE else DK

        block = stack.enter_context(nc.Block())

        @block.sync
        def _(sp):
            def load(r, s):
                sp.dma_start(x_in[s][:, :], x[r * STREAMS + s, :, :]).then_inc(x_loaded[s], 16)
                sp.dma_start(c_in[s][:, :], ctx_in[r * STREAMS + s, :, :]).then_inc(c_loaded[s], 16)
                sp.dma_start(mask_bs_i[s][:, :], mask_bs[bass.ds(r * STREAMS + s, 1), :]).then_inc(m_loaded[s], 16)

            def load_weight(name):
                rows, n = W_ROWS.get(name, D), dict(WEIGHTS)[name]
                dst = W[:, W_AT[name]:W_AT[name] + rows // P * n].rearrange("p (k n) -> p k n", n=n)
                sp.dma_start(dst, weights[name].rearrange("(k p) n -> p k n", p=P)).then_inc(w_in[name], 16)

            for s in range(STREAMS):
                sp.sem_inc(stored[s], 16)
            sp.dma_start(Pr[0][:, :], consts[:, 0:HU * P]).then_inc(consts_in, 16)
            sp.dma_start(Pr[1][:, 0:C_COLS - HU * P], consts[:, HU * P:C_COLS]).then_inc(consts_in, 16)
            load(0, 0)
            for name in ("k0", "q0", "v0"):
                load_weight(name)
            for s in range(1, STREAMS):
                load(0, s)
            early = ROW_AT[ROWS[ROWS_EARLY][0]]
            sp.dma_start(RV[:, 0:early], row_vec[0:1, 0:early].to_broadcast([P, early])).then_inc(rows_in, 16)
            sp.dma_start(CB[:, :], col_bias[:, :]).then_inc(cols_in, 16)
            sp.dma_start(PT[0][:, 0:P].bitcast(I32), mask_ss[:, :]).then_inc(masks_in, 16)
            for name, _n in WEIGHTS[3:8]:
                load_weight(name)
            sp.dma_start(RV[:, early:ROW_COLS],
                         row_vec[0:1, early:ROW_COLS].to_broadcast([P, ROW_COLS - early])).then_inc(rows_late_in, 16)
            for name, _n in WEIGHTS[8:]:
                load_weight(name)

            def store(r, s):
                value = sp.to_reg(r * COUNT["norm"] + (AT["norm"][("att", 5, s)] + 1))
                sp.wait_ge(consts_in, 32)
                sp.wait_ge(normed, value)
                sp.dma_start(out[r * STREAMS + s, :, :], X[s][:, :]).then_inc(stored[s], 16)

            with sp.Fori(1, ROUNDS) as r:
                for s in range(STREAMS):
                    value = sp.to_reg((r - 1) * STREAMS + (s + 1))
                    sp.wait_ge(consts_in, 32)
                    sp.wait_ge(cm_done, value)
                    load(r, s)
                for s in range(STREAMS):
                    store(r - 1, s)
            for s in range(STREAMS):
                store(ROUNDS - 1, s)
            for s in range(STREAMS):
                sp.wait_ge(stored[s], 16 * ROUNDS + 16)

        @block.tensor
        def _(pe):
            pe.wait_ge(ready_act, 1)
            pe.wait_ge(ready_dve, 1)
            with pe.Fori(0, ROUNDS) as r:
                wait, wait_nth = waiter(pe, r)

                def free_tile(it):
                    i = AT["tile"][it]
                    if i >= len(M):
                        old = INDEX["tile"][i - len(M)]
                        if old[0] in BY_ACT:
                            wait(tile_act, "tile_act", old)
                        else:
                            wait(tile_dve, "tile_dve", old)
                    else:
                        wait_nth(tile_act, "tile_act", -1)
                        wait_nth(tile_dve, "tile_dve", -1)

                def product(dst, lhsTs, rhss):
                    for k, (a, b) in enumerate(zip(lhsTs, rhss)):
                        last = pe.matmul(dst, a, b, start=(k == 0), stop=(k == len(lhsTs) - 1))
                    return last

                def turn(dst, src, n):
                    for i in range(n):
                        last = pe.transpose(dst[:, i * P:(i + 1) * P], src[:, i * P:(i + 1) * P], ident[:, :])
                    return last

                def by_weight(it, name, src, tiles, first=0):
                    pe.wait_ge(w_in[name], 16)
                    for j in range(tiles):
                        m = (first + j) * P
                        last = product(tile_of(it)[:, j * P:(j + 1) * P],
                                       [weight(name, k, m, m + P) for k in range(KC)],
                                       [src[:, k * P:(k + 1) * P] for k in range(KC)])
                    last.then_inc(tile_full, 1)

                def by_tokens(it, name, src, n, at=0, chunks=KC):
                    pe.wait_ge(w_in[name], 16)
                    product(tile_of(it)[:, 0:n], [src[:, k * P:(k + 1) * P] for k in range(chunks)],
                            [weight(name, k, at, at + n) for k in range(chunks)]).then_inc(tile_full, 1)

                for it in ORDER:
                    kind = it[0]
                    if kind in BY_ACT | BY_DVE:
                        free_tile(it)
                    if kind == "XT":
                        j, s = it[1:]
                        if j == 0:
                            pe.wait_ge(x_loaded[s], r * 16 + 16)
                            src = x_in[s]
                        else:
                            wait(normed, "norm", (*XT_AFTER[j], s))
                            src = X[s]
                        turn(tile_of(it), src, KC).then_inc(tile_full, 1)
                    elif kind == "CT":
                        s = it[1]
                        pe.wait_ge(c_loaded[s], r * 16 + 16)
                        turn(tile_of(it), c_in[s], KC).then_inc(tile_full, 1)
                    elif kind == "CM":
                        s = it[1]
                        wait(cm_done, "stream", s)
                        turn(tile_of(it), O[s % 2], KC).then_inc(tile_full, 1)
                    elif kind in ("K", "V"):
                        _, a, s, c = it
                        if a in (0, 2):
                            wait(tile_act, "tile_act", ("XT", XT_FOR_ATT[a], s))
                            src = XT[s]
                        elif a == 1:
                            wait(tile_act, "tile_act", ("CM", s))
                            src = CmT[s % 2]
                        else:
                            wait(tile_act, "tile_act", ("CT", s))
                            src = CT[s]
                        if kind == "K":
                            by_weight(it, f"k{a}", src, 4 if a == WIDE else 2, 4 * c)
                        else:
                            by_tokens(it, f"v{a}", src, 512 if a == WIDE else D, 512 * c)
                    elif kind == "Q":
                        _, a, s, c = it
                        wait(tile_act, "tile_act", ("XT", XT_FOR_ATT[a], s))
                        by_weight(it, f"q{a}", XT[s], 4 if a == WIDE else 2, 4 * c)
                    elif kind == "L":
                        _, a, s, c = it
                        wait(q0_done, "q0", (a, s))
                        wait(tile_dve, "tile_dve", ("K", a, s, 0))
                        pe.matmul(tile_of(it)[0:HU, 0:P], q0[s % 2][:, c, :], KTp[s % 2][:, c * P:(c + 1) * P],
                                  start=True, stop=True).then_inc(tile_full, 1)
                    elif kind == "S":
                        n = it[1]
                        a, s, c = unit(n)
                        wait_nth(probs, "unit", n - 2)
                        q, k, sc = QT[s % 2], KT[s % 2], SC[c]
                        if a == WIDE:
                            wait(tile_act, "tile_act", ("Q", a, s, c))
                            wait(tile_dve, "tile_dve", ("K", a, s, c))
                            for j in range(HU):
                                rows, cols = 64 * (j % 2), (4 * c + j // 2) * P
                                at = (4 * (j % 2) + j // 2) * P
                                last = pe.matmul(sc[:, at:at + P], q[rows:rows + 64, cols:cols + P],
                                                 k[rows:rows + 64, cols:cols + P], start=True, stop=True,
                                                 skip_group_check=True)
                            last.then_inc(scores, 1)
                            continue
                        wait(tile_act, "tile_act", ("Q", a, s, 0))
                        wait(tile_dve, "tile_dve", ("K", a, s, 0))
                        if a in MASKED_BY_LENGTH:
                            wait(len_mask, "length", (a, s, c))
                        for u in range(2):
                            terms = [(q[64 * u:64 * u + 64, c * P:(c + 1) * P],
                                      k[64 * u:64 * u + 64, c * 512:(c + 1) * 512])]
                            heads = lambda mask: mask.unsqueeze(1).to_broadcast([mask.shape[0], 4, P])
                            if a == 0:
                                terms.append((ident_b[:, :], heads(causal_b[:, :])))
                            if a in MASKED_BY_LENGTH:
                                terms.append((ones_b[:, :], LB[c][:, u * 512:(u + 1) * 512]))
                            if a == 2:
                                terms.append((ident_b[:, :], heads(mask_ss_b[:, :])))
                            if a == 3:
                                wait(mask_done, "stream", s)
                                terms.append((ones_b[0:1, :], heads(mask_bs_b[s][:, :])))
                            last = product(sc[:, u * 512:(u + 1) * 512], *zip(*terms))
                        last.then_inc(scores, 1)
                    elif kind == "T":
                        _, n, u = it
                        if unit(n)[0] == WIDE:
                            wait(wide_norm, "wide", n)
                        else:
                            wait(probs, "unit", n)
                        turn(tile_of(it), Pr[n % 2][:, u * 512:(u + 1) * 512], 4).then_inc(tile_full, 1)
                    elif kind == "PV":
                        _, n, u = it
                        a, s, c = unit(n)
                        wait(tile_act, "tile_act", ("T", n, u))
                        if c == 0 and u == 0 or a == WIDE:
                            if n == 0:
                                wait_nth(context_out, "ctx", -1)
                            else:
                                before = [m for m in INDEX["ctx"] if m < n][-1]
                                wait(context_out, "ctx", before)
                        if n % 2 == 0 and u == 0 or a == WIDE:
                            wait(tile_dve, "tile_dve", ("V", a, s, c if a == WIDE else 0))
                        for e in range(4):
                            rhs = PT[u][:, e * P:(e + 1) * P]
                            if a == WIDE:
                                h = HU * c + 2 * e + u
                                last = pe.matmul(OTp[64 * u:64 * u + 64, e * P:(e + 1) * P],
                                                 V64[s % 2][:, h * DK2:(h + 1) * DK2],
                                                 rhs, start=True, stop=True, skip_group_check=True)
                            else:
                                h = HU * c + 4 * u + e
                                cols = (2 * c + u) * P
                                last = pe.matmul(OTp[32 * e:32 * e + 32, cols:cols + P], V16[s % 2][:, h, :], rhs,
                                                 start=True, stop=True, skip_group_check=True)
                        last.then_inc(context, 1)
                    elif kind == "E1":
                        _, a, s, _c = it
                        wait(context_out, "ctx", 8 * a + 2 * s + 1)
                        turn(tile_of(it), OT[s % 2], 4).then_inc(tile_full, 1)
                    elif kind == "E2":
                        _, a, s, _c = it
                        wait(tile_dve, "tile_dve", ("E1", a, s, 0))
                        turn(tile_of(it), O[s % 2], KC).then_inc(tile_full, 1)
                    elif kind == "E3":
                        _, a, s, _c = it
                        if a == WIDE:
                            wait(context_out, "ctx", 8 * a + 2 * s + 1)
                            by_tokens(it, f"o{a}", OT[s % 2], D, chunks=HEADS * DK2 // P)
                        else:
                            wait(tile_act, "tile_act", ("E2", a, s, 0))
                            by_tokens(it, f"o{a}", OnT[s % 2], D)
                    elif kind == "F1":
                        _, a, s, c = it
                        wait(tile_act, "tile_act", ("XT", 2 if a == 1 else 5, s))
                        if a == 1:
                            by_weight(it, "f0", XT[s], FF0 // P)
                        else:
                            by_weight(it, "f1", XT[s], 4, 4 * c)
                    elif kind == "F2":
                        _, a, s, _c = it
                        wait(tile_act, "tile_act", ("F1", a, s, 0 if a == 1 else 1))
                        by_tokens(it, "g0" if a == 1 else "g1", QT[s % 2], D, chunks=(FF0 if a == 1 else FF1) // P)

        @block.scalar
        def _(act):
            act.wait_ge(consts_in, 32)
            act.activation(ident[:, :], Pr[0][:, C_AT["ident"]:C_AT["ident"] + P], ACT.Copy)
            act.activation(ident_b[:, :], Pr[0][:, C_AT["ident"]:C_AT["ident"] + P], ACT.Copy)
            act.activation(causal_b[:, :], Pr[0][:, C_AT["causal"]:C_AT["causal"] + P], ACT.Copy).then_inc(ready_act, 1)
            act.sem_inc(tile_act, 1)
            act.sem_inc(probs, 1)
            act.sem_inc(context_out, 1)
            act.wait_ge(ready_dve, 1)
            act.wait_ge(cols_in, 16)
            act.wait_ge(cols_scaled, 1)
            with act.Fori(0, ROUNDS) as r:
                wait, wait_nth = waiter(act, r)
                for it in ORDER:
                    kind = it[0]
                    if kind in BY_ACT:
                        wait(tile_full, "tile", it)
                    if kind == "XT":
                        s = it[2]
                        act.activation(XT[s][:, :], tile_of(it)[:, 0:D], ACT.Copy).then_inc(tile_act, 1)
                    elif kind == "CT":
                        act.activation(CT[it[1]][:, :], tile_of(it)[:, 0:D], ACT.Copy).then_inc(tile_act, 1)
                    elif kind == "CM":
                        act.activation(CmT[it[1] % 2], tile_of(it)[:, 0:D], ACT.Copy).then_inc(tile_act, 1)
                    elif kind == "E2":
                        act.activation(OnT[it[2] % 2][:, :], tile_of(it)[:, 0:D], ACT.Copy).then_inc(tile_act, 1)
                    elif kind == "Q":
                        _, a, s, c = it
                        scale = float(width(a)) ** -0.5
                        if a in (0, 1):
                            last = act.activation(QT[s % 2][:, 0:D], tile_of(it)[:, 0:D], ACT.Copy, scale=scale)
                        else:
                            for j in range(4 if a == WIDE else 2):
                                b = CB_AT[f"q{a}"] + 4 * c + j
                                last = act.activation(QT[s % 2][:, (4 * c + j) * P:(4 * c + j + 1) * P],
                                                      tile_of(it)[:, j * P:(j + 1) * P], ACT.Identity, bias=CB[:, b:b + 1],
                                                      scale=scale)
                        last.then_inc(tile_act, 1)
                    elif kind == "F1":
                        _, a, s, c = it
                        for j in range(2 if a == 1 else 4):
                            b = CB_AT["f0" if a == 1 else "f1"] + 4 * c + j
                            last = act.activation(QT[s % 2][:, (4 * c + j) * P:(4 * c + j + 1) * P],
                                                  tile_of(it)[:, j * P:(j + 1) * P], ACT.Relu if a == 1 else ACT.Gelu,
                                                  bias=CB[:, b:b + 1])
                        last.then_inc(tile_act, 1)
                    elif kind == "A":
                        n = it[1]
                        wait(maxima, "unit", n)
                        for h in range(HU):
                            last = act.activation(Pr[n % 2][:, h * P:(h + 1) * P], SC[n % 2][:, h * P:(h + 1) * P],
                                                  ACT.Exp, bias=nmax[n % 2][:, h:h + 1])
                        last.then_inc(probs, 1)
                    elif kind == "T":
                        act.activation(PT[it[2]][:, :], tile_of(it)[:, :], ACT.Copy).then_inc(tile_act, 1)
                    elif kind == "PV" and it[2] == 1 and it[1] in AT["ctx"]:
                        n = it[1]
                        a, s, c = unit(n)
                        wait(context, "half", (n, 1))
                        at = 512 * c if a == WIDE else 0
                        act.activation(OT[s % 2][:, at:at + 512], OTp[:, :], ACT.Copy).then_inc(context_out, 1)

        @block.vector
        def _(dve):
            dve.wait_ge(consts_in, 32)
            late = HU * P
            for dst, name, rows, n in ((khead, "khead", P, 4), (qhead, "qhead", P, HU), (iota, "iota", HU, P)):
                dve.tensor_copy(dst[:, :], Pr[0][0:rows, C_AT[name]:C_AT[name] + n])
            at = C_AT["hsel"]
            dve.tensor_copy(hsel_b[:, 0:late - at], Pr[0][0:HU, at:late])
            dve.tensor_copy(hsel_b[:, late - at:HU * P], Pr[1][0:HU, 0:C_COLS - late])
            dve.memset(ones_b[:, :], 1.0)
            dve.memset(half[:, :], -0.5)
            dve.wait_ge(masks_in, 16)
            dve.tensor_scalar(mask_ss_b[:, :], PT[0][:, 0:P].bitcast(I32), 0.0, -BIG, ALU.is_equal, ALU.mult)
            for i in range(2):
                dve.memset(V16[i][:, :, DK:DK + 1], 1.0)
                last = dve.memset(V16[i][:, :, DK + 1:32], 0.0)
            last.then_inc(ready_dve, 1)
            dve.sem_inc(tile_dve, 1)
            dve.wait_ge(rows_in, 16)
            dve.wait_ge(cols_in, 16)
            for name, n in COLUMN_BIASES:
                if name[0] == "q":
                    b = CB[:, CB_AT[name]:CB_AT[name] + n // P]
                    last = dve.tensor_scalar(b, b, float(width(int(name[1]))) ** -0.5, None, ALU.mult)
            last.then_inc(cols_scaled, 1)

            with dve.Fori(0, ROUNDS) as r:
                wait, wait_nth = waiter(dve, r)

                def norm(what, a, s):
                    key, y = (what, a, s), O[s % 2]
                    name = LN_OF[(what, a)]
                    dve.bn_stats(stats[:, :], y[:, :]).then_inc(stats_done, 1)
                    value = dve.to_reg(r * COUNT["norm"] + (AT["norm"][key] + 1))
                    dve.wait_ge(rows_in, 16)
                    dve.wait_ge(stats_done, value)
                    dve.bn_aggr(mv[:, :], stats[:, :]).then_inc(var_done, 1)
                    wait(var_done, "norm", key)
                    i = AT["norm"][key] % 2
                    dve.tensor_scalar(rstd[i][:, :], mv[:, 1:2], EPS, None, ALU.add).then_inc(eps_done, 1)
                    dve.scalar_tensor_tensor(out=xc[:, :], in0=y[:, :], scalar=mv[:, 0:1], in1=row(name + "g"),
                                             op0=ALU.subtract, op1=ALU.mult).then_inc(centred, 1)
                    wait(centred, "norm", key)
                    wait(rstd_done, "norm", key)
                    if (what, a) == ("att", 0):
                        dve.wait_ge(stored[s], r * 16 + 16)
                    dve.scalar_tensor_tensor(out=X[s][:, :], in0=xc[:, :], scalar=rstd[i][:, 0:1],
                                             in1=row(name + "b"), op0=ALU.mult, op1=ALU.add).then_inc(normed, 1)

                for it in ORDER:
                    kind = it[0]
                    if kind in BY_DVE:
                        wait(tile_full, "tile", it)
                    if kind == "XT" and it[1] == 0:
                        s = it[2]
                        dve.wait_ge(x_loaded[s], r * 16 + 16)
                        dve.tensor_reduce(absmax[:, :], x_in[s][:, :], AX_X, ALU.max,
                                          apply_absolute_value=True).then_inc(abs0, 1)
                        wait(abs0, "stream", s)
                        dve.tensor_scalar(seen0[s][:, :], absmax[:, :], 0.0, None, ALU.is_gt).then_inc(seen0_done, 1)
                        dve.wait_ge(m_loaded[s], r * 16 + 16)
                        dve.tensor_scalar(mask_bs_b[s][:, :], mask_bs_i[s][:, :], 0.0, -BIG, ALU.is_equal,
                                          ALU.mult).then_inc(mask_done, 1)
                    elif kind == "K":
                        _, a, s, c = it
                        k, t = KT[s % 2], tile_of(it)
                        if a == WIDE:
                            b = CB_AT[f"k{a}"] + 4 * c
                            last = dve.tensor_tensor(k[:, c * 512:(c + 1) * 512].rearrange("p (j t) -> p j t", t=P),
                                                     t[:, :].rearrange("p (j t) -> p j t", t=P),
                                                     CB[:, b:b + 4].unsqueeze(2).to_broadcast([P, 4, P]), ALU.add)
                        else:
                            for j in range(2):
                                dst = k[:, j * 512:(j + 1) * 512].rearrange("p (e t) -> p e t", t=P)
                                src = t[:, j * P:(j + 1) * P].unsqueeze(1).to_broadcast([P, 4, P])
                                own = khead[:, :].unsqueeze(2).to_broadcast([P, 4, P])
                                if a in (0, 1):
                                    last = dve.tensor_tensor(dst, src, own, ALU.mult)
                                else:
                                    b = CB_AT[f"k{a}"] + j
                                    last = dve.scalar_tensor_tensor(out=dst, in0=src, scalar=CB[:, b:b + 1], in1=own,
                                                                    op0=ALU.add, op1=ALU.mult)
                            if a in MASKED_BY_LENGTH:
                                last = dve.tensor_copy(KTp[s % 2], t[:, 0:D])
                        last.then_inc(tile_dve, 1)
                    elif kind == "Q" and it[1] in MASKED_BY_LENGTH:
                        _, a, s, c = it
                        wait(tile_act, "tile_act", it)
                        first = QT[s % 2][:, 0:D].rearrange("p (c t) -> p c t", t=P)[:, :, 0:1]
                        dve.tensor_tensor(q0[s % 2][:, :, :], first.to_broadcast([P, 2, HU]),
                                          qhead[:, :].unsqueeze(1).to_broadcast([P, 2, HU]), ALU.mult).then_inc(q0_done, 1)
                    elif kind == "V":
                        _, a, s, c = it
                        if a == WIDE:
                            last = dve.tensor_tensor(V64[s % 2][:, 512 * c:512 * (c + 1)], tile_of(it)[:, :],
                                                     row("v4", 512, 512 * c), ALU.add)
                        else:
                            src = tile_of(it)[:, 0:D].rearrange("p (h d) -> p h d", d=DK)
                            dst = V16[s % 2][:, :, 0:DK]
                            if a in (0, 1):
                                last = dve.tensor_copy(dst, src)
                            else:
                                if a == 2 and s == 0:
                                    dve.wait_ge(rows_late_in, 16)
                                last = dve.tensor_tensor(dst, src, row(f"v{a}").rearrange("p (h d) -> p h d", d=DK),
                                                         ALU.add)
                        last.then_inc(tile_dve, 1)
                    elif kind == "L":
                        _, a, s, c = it
                        key = (a, s, c)
                        dve.tensor_scalar(ne[:, :], tile_of(it)[0:HU, 0:P], 0.0, None, ALU.not_equal).then_inc(tile_dve, 1)
                        wait(tile_dve, "tile_dve", it)
                        dve.tensor_reduce(cnt[:, :], ne[:, :], AX_X, ALU.add).then_inc(len_cnt, 1)
                        wait(len_cnt, "length", key)
                        dve.reciprocal(crec[:, :], cnt[:, :]).then_inc(len_rec, 1)
                        wait(len_rec, "length", key)
                        dve.tensor_scalar(lval[:, :], crec[:, :], cnt[:, 0:1], -BIG, ALU.mult, ALU.mult).then_inc(len_val, 1)
                        wait(len_val, "length", key)
                        dve.tensor_scalar(lrow[:, :], iota[:, :], cnt[:, 0:1], lval[:, 0:1], ALU.is_ge,
                                          ALU.mult).then_inc(len_row, 1)
                        wait(len_row, "length", key)
                        dve.tensor_tensor(LB[c].rearrange("p (h t) -> p h t", t=P),
                                          hsel_b[:, :].rearrange("p (h t) -> p h t", t=P),
                                          lrow[:, :].unsqueeze(1).to_broadcast([HU, HU, P]), ALU.mult).then_inc(len_mask, 1)
                    elif kind == "S":
                        n = it[1]
                        wait(scores, "unit", n)
                        i = n % 2
                        dve.tensor_reduce(nmax[i][:, :], SC[i][:, :].rearrange("p (h t) -> p h t", t=P), AX_X, ALU.max,
                                          negate=True).then_inc(maxima, 1)
                    elif kind == "A" and unit(it[1])[0] == WIDE:
                        n = it[1]
                        i = n % 2
                        wait(probs, "unit", n)
                        dve.tensor_reduce(wsum[i][:, :], Pr[i][:, :].rearrange("p (h t) -> p h t", t=P), AX_X,
                                          ALU.add).then_inc(wide_sum, 1)
                        wait(wide_sum, "wide", n)
                        dve.reciprocal(wrec[i][:, :], wsum[i][:, :]).then_inc(wide_rec, 1)
                    elif kind == "E1":
                        _, a, s, _c = it
                        t = tile_of(it)[:, :].rearrange("p (h d) -> p h d", d=32)
                        rec = rsum[s % 2]
                        key = (a, s, 0)
                        dve.reciprocal(rec[:, :].unsqueeze(2), t[:, :, DK:DK + 1]).then_inc(recip_done, 1)
                        wait(recip_done, "e1", key)
                        if a in (0, 1):
                            if a == 0:
                                wait(seen0_done, "stream", s)
                            else:
                                wait(seen1_done, "stream", s)
                            dve.tensor_scalar(rec[:, :], rec[:, :], (seen0, seen1)[a][s][:, 0:1], None,
                                              ALU.mult).then_inc(recip_masked, 1)
                            wait(recip_masked, "residual", (a, s))
                        dve.tensor_tensor(O[s % 2][:, :].rearrange("p (h d) -> p h d", d=DK), t[:, :, 0:DK],
                                          rec[:, :].unsqueeze(2).to_broadcast([P, HEADS, DK]), ALU.mult)\
                           .then_inc(tile_dve, 1)
                        if a in (0, 1):
                            wait(tile_dve, "tile_dve", it)
                            dve.tensor_tensor(O[s % 2][:, :], O[s % 2][:, :], (x_in if a == 0 else X)[s][:, :],
                                              ALU.add).then_inc(summed, 1)
                            wait(summed, "residual", (a, s))
                            norm("att", a, s)
                        if a == 0:
                            wait(normed, "norm", ("att", 0, s))
                            dve.tensor_reduce(absmax[:, :], X[s][:, :], AX_X, ALU.max,
                                              apply_absolute_value=True).then_inc(abs1, 1)
                            wait(abs1, "stream", s)
                            dve.tensor_scalar(seen1[s][:, :], absmax[:, :], 0.0, None, ALU.is_gt).then_inc(seen1_done, 1)
                            wait(seen1_done, "stream", s)
                            dve.wait_ge(c_loaded[s], r * 16 + 16)
                            dve.tensor_scalar(O[s % 2][:, :], c_in[s][:, :], seen1[s][:, 0:1], None,
                                              ALU.mult).then_inc(cm_done, 1)
                    elif kind == "E3":
                        _, a, s, _c = it
                        wait(xb_done, "xb", (f"o{a}", s))
                        dve.tensor_tensor(O[s % 2][:, :], tile_of(it)[:, 0:D], XB[s][:, :], ALU.add).then_inc(tile_dve, 1)
                        wait(tile_dve, "tile_dve", it)
                        norm("att", a, s)
                    elif kind == "F2":
                        _, a, s, _c = it
                        wait(xb_done, "xb", ("g0" if a == 1 else "g1", s))
                        if a == 1:
                            dve.scalar_tensor_tensor(out=O[s % 2][:, :], in0=tile_of(it)[:, 0:D], scalar=seen0[s][:, 0:1],
                                                     in1=XB[s][:, :], op0=ALU.mult, op1=ALU.add).then_inc(tile_dve, 1)
                        else:
                            dve.tensor_tensor(O[s % 2][:, :], tile_of(it)[:, 0:D], XB[s][:, :],
                                              ALU.add).then_inc(tile_dve, 1)
                        wait(tile_dve, "tile_dve", it)
                        norm("ff", a, s)

        @block.gpsimd
        def _(pool):
            pool.wait_ge(ready_dve, 1)
            pool.wait_ge(rows_in, 16)
            with pool.Fori(0, ROUNDS) as r:
                wait, wait_nth = waiter(pool, r)

                def after_norm(what, a, s):
                    key = (what, a, s)
                    i = AT["norm"][key] % 2
                    wait(eps_done, "norm", key)
                    pool.tensor_tensor(rstd[i][:, :], rstd[i][:, :], half[:, :], ALU.pow).then_inc(rstd_done, 1)
                    if (what, a) not in XB_AFTER:
                        return
                    name = XB_AFTER[(what, a)]
                    wait(normed, "norm", key)
                    if name == "g0":
                        pool.tensor_tensor(XB[s][:, :], row("g0"), seen0[s][:, 0:1].to_broadcast([P, D]),
                                           ALU.mult).then_inc(xb_half, 1)
                        wait(xb_half, "stream", s)
                        pool.tensor_tensor(XB[s][:, :], XB[s][:, :], X[s][:, :], ALU.add).then_inc(xb_done, 1)
                    else:
                        if name == "o2" and s == 0:
                            pool.wait_ge(rows_late_in, 16)
                        pool.tensor_tensor(XB[s][:, :], X[s][:, :], row(name), ALU.add).then_inc(xb_done, 1)

                for it in ORDER:
                    kind = it[0]
                    if kind == "A" and unit(it[1])[0] == WIDE:
                        n = it[1]
                        i = n % 2
                        wait(wide_rec, "wide", n)
                        p = Pr[i][:, :].rearrange("p (h t) -> p h t", t=P)
                        pool.tensor_tensor(p, p, wrec[i][:, :].unsqueeze(2).to_broadcast([P, HU, P]),
                                           ALU.mult).then_inc(wide_norm, 1)
                    elif kind == "E1" and it[1] in (0, 1):
                        after_norm("att", it[1], it[2])
                    elif kind == "E3":
                        after_norm("att", it[1], it[2])
                    elif kind == "F2":
                        after_norm("ff", it[1], it[2])


def shape_constants():
    c = np.zeros((P, C_COLS), np.float32)
    p = np.arange(P)[:, None]
    t = np.arange(P)[None, :]
    c[:, C_AT["ident"]:][:, :P] = p == t
    c[:, C_AT["causal"]:][:, :P] = np.where(t > p, -BIG, 0.0)
    c[:, C_AT["khead"]:][:, :4] = p % 64 // DK == np.arange(4)[None, :]
    c[:, C_AT["qhead"]:][:, :HU] = p // DK == np.arange(HU)[None, :]
    c[:, C_AT["iota"]:][:, :P] = t
    c[:, C_AT["hsel"]:][:, :HU * P] = np.repeat(p % HU == np.arange(HU)[None, :], P, axis=1)
    return c


def kernel(**inputs):
    import concourse.bacc as bacc
    from concourse.bass_utils import run_bass_kernel_spmd as run

    v = {k: np.asarray(a) for k, a in inputs.items()}
    heads_last = lambda w: np.ascontiguousarray(np.transpose(w, (1, 0, 2)).reshape(D, -1))
    L0, L1, L2, L3 = "L0_xattn_", "L1_xattn_", "L2_xattn_", "L3_xattn_"
    qkv = v[L3 + "W_qkv"]
    w = {
        "q0": heads_last(v[L0 + "Wq1"]), "k0": heads_last(v[L0 + "Wk1"]), "v0": heads_last(v[L0 + "Wv1"]),
        "q1": heads_last(v[L0 + "Wq2"]), "k1": heads_last(v[L0 + "Wk2"]), "v1": heads_last(v[L0 + "Wv2"]),
        "f0": v[L0 + "fc1_w"].T, "g0": v[L0 + "fc2_w"].T,
        "q2": v[L1 + "self_wq"], "k2": v[L1 + "self_wk"], "v2": v[L1 + "self_wv"], "o2": v[L1 + "self_wo"],
        "q3": v[L1 + "cross_wq"], "k3": v[L1 + "cross_wk"], "v3": v[L1 + "cross_wv"], "o3": v[L1 + "cross_wo"],
        "f1": v[L1 + "ff_w1"], "g1": v[L1 + "ff_w2"],
        "q4": v[L2 + "Wq"], "k4": v[L2 + "Wk"], "v4": v[L2 + "Wv"], "o4": v[L2 + "Wo"],
        "q5": qkv[:D].T, "k5": qkv[D:2 * D].T, "v5": qkv[2 * D:].T, "o5": v[L3 + "W_o"].T,
    }
    b3 = v[L3 + "b_qkv"]
    cb = {"f0": v[L0 + "fc1_b"], "q2": v[L1 + "self_bq"], "k2": v[L1 + "self_bk"], "q3": v[L1 + "cross_bq"],
          "k3": v[L1 + "cross_bk"], "f1": v[L1 + "ff_b1"], "q4": v[L2 + "bq"], "k4": v[L2 + "bk"],
          "q5": b3[:D], "k5": b3[D:2 * D]}
    rows = {"ln0g": v[L0 + "ln1_g"], "ln0b": v[L0 + "ln1_b"], "ln1g": v[L0 + "ln2_g"], "ln1b": v[L0 + "ln2_b"],
            "lnfg": v[L0 + "ln3_g"], "lnfb": v[L0 + "ln3_b"], "g0": v[L0 + "fc2_b"], "v2": v[L1 + "self_bv"],
            "o2": v[L1 + "self_bo"], "ln2g": v[L1 + "n1_g"], "ln2b": v[L1 + "n1_b"], "v3": v[L1 + "cross_bv"],
            "o3": v[L1 + "cross_bo"], "ln3g": v[L1 + "n2_g"], "ln3b": v[L1 + "n2_b"], "g1": v[L1 + "ff_b2"],
            "lnhg": v[L1 + "n3_g"], "lnhb": v[L1 + "n3_b"], "v4": v[L2 + "bv"], "o4": v[L2 + "bo"],
            "ln4g": v[L2 + "gamma"], "ln4b": v[L2 + "beta"], "v5": b3[2 * D:], "o5": v[L3 + "b_o"],
            "ln5g": v[L3 + "ln_gamma"], "ln5b": v[L3 + "ln_beta"]}
    arrays = {f"w_{name}": np.ascontiguousarray(w[name]) for name, _ in WEIGHTS}
    arrays["col_bias"] = np.ascontiguousarray(
        np.concatenate([cb[name].reshape(-1, P).T for name, _ in COLUMN_BIASES], axis=1))
    arrays["row_vec"] = np.ascontiguousarray(np.concatenate([rows[name] for name, _ in ROWS])[None, :])
    arrays["consts"] = shape_constants()
    arrays["x"] = np.ascontiguousarray(v["x"])
    arrays["ctx_in"] = np.ascontiguousarray(v["ctx_1024"])
    arrays["mask_ss"] = np.ascontiguousarray(v["mask_SxS2_ik0"])
    arrays["mask_bs"] = np.ascontiguousarray(v["mask_Bx1x1xS2_if1"].reshape(BATCH, SEQ))

    nc = bacc.Bacc("TRN2", target_bir_lowering=False, num_devices=1)
    ap = {k: nc.dram_tensor(k, a.shape, mybir.dt.from_np(a.dtype), kind="ExternalInput").ap() for k, a in arrays.items()}
    out = nc.dram_tensor("out", (BATCH, SEQ, D), F32, kind="ExternalOutput").ap()
    build(nc, ap["x"], ap["ctx_in"], ap["mask_ss"], ap["mask_bs"], {name: ap[f"w_{name}"] for name, _ in WEIGHTS},
          ap["col_bias"], ap["row_vec"], ap["consts"], out)
    r = run(nc, [arrays], core_ids=[0])
    return r.results[0]["out"]
```

```python
from contextlib import ExitStack

import numpy as np
import concourse.bass as bass
from concourse import mybir

ALU = mybir.AluOpType
ACT = mybir.ActivationFunctionType
AX_X = mybir.AxisListType.X
F32 = mybir.dt.float32
F32R = mybir.dt.float32r
BF16 = mybir.dt.bfloat16
I32 = mybir.dt.int32

P = 128
BATCH, SEQ, D, HEADS = 32, 128, 256, 16
KC = D // P
DK, DK2 = 16, 64
FF0, FF1 = 256, 1024
LANES = 4
GROUPS = 2
STREAMS = GROUPS * LANES
ROUNDS = BATCH // STREAMS
ATTS = 6
HU = HEADS // 2
GROUP_UNITS = ATTS * LANES * 2
UNITS = GROUPS * GROUP_UNITS
BIG = 2.0 ** 100
EPS = 1e-5
WIDE = 4
MASKED_BY_LENGTH = (0, 1)

WEIGHTS = [("q0", D), ("k0", D), ("v0", D), ("q1", D), ("k1", D), ("v1", D), ("f0", FF0), ("g0", D),
           ("q2", D), ("k2", D), ("v2", D), ("o2", D), ("q3", D), ("k3", D), ("v3", D), ("o3", D),
           ("f1", FF1), ("g1", D), ("q4", HEADS * DK2), ("k4", HEADS * DK2), ("v4", HEADS * DK2), ("o4", D),
           ("q5", D), ("k5", D), ("v5", D), ("o5", D)]
W_ROWS = {"g1": FF1, "o4": HEADS * DK2}
COLUMN_BIASES = [("f0", FF0), ("q2", D), ("k2", D), ("q3", D), ("k3", D), ("f1", FF1),
                 ("q4", HEADS * DK2), ("k4", HEADS * DK2), ("v4", HEADS * DK2), ("q5", D), ("k5", D)]
ROWS = [("ln0g", D), ("ln0b", D), ("ln1g", D), ("ln1b", D), ("lnfg", D), ("lnfb", D), ("g0", D),
        ("v2", D), ("o2", D), ("ln2g", D), ("ln2b", D), ("v3", D), ("o3", D), ("ln3g", D), ("ln3b", D),
        ("g1", D), ("lnhg", D), ("lnhb", D), ("o4", D), ("ln4g", D), ("ln4b", D),
        ("v5", D), ("o5", D), ("ln5g", D), ("ln5b", D)]
ROWS_EARLY = 7


def offsets(parts, width=lambda n: n):
    at, out = 0, {}
    for name, n in parts:
        out[name] = at
        at += width(n)
    return out, at


W_AT, W_COLS = {}, 0
for _name, _n in WEIGHTS:
    W_AT[_name] = W_COLS
    W_COLS += W_ROWS.get(_name, D) // P * _n
CB_AT, CB_COLS = offsets(COLUMN_BIASES, lambda n: n // P)
ROW_AT, ROW_COLS = offsets(ROWS)

CONSTS = [("ident", P), ("causal", P), ("khead", 4), ("qhead", HU), ("iota", P)]
C_AT, C_COLS = offsets(CONSTS)

LN_OF = {("att", 0): "ln0", ("att", 1): "ln1", ("ff", 1): "lnf", ("att", 2): "ln2", ("att", 3): "ln3",
         ("ff", 3): "lnh", ("att", 4): "ln4", ("att", 5): "ln5"}
XT_AFTER = [None, ("att", 0), ("att", 1), ("ff", 1), ("att", 2), ("att", 3), ("ff", 3), ("att", 4)]
XT_FOR_ATT = [0, 1, 3, 4, 6, 7]


def unit(n):
    return n % GROUP_UNITS // (2 * LANES), n // GROUP_UNITS * LANES + n // 2 % LANES, n % 2


def first_unit(a, s):
    return s // LANES * GROUP_UNITS + (a * LANES + s % LANES) * 2


STEP = [("T", 0), ("T", 1), 0, "A", 1, "S", 2, ("PV", 0), ("PV", 1), 3]
PLAN = {
    -1: [(4, 0, "XT", 0), (4, 3, "K"), (5, 1, "CT"), (5, 3, "Q"), (6, 3, "L"), (7, 1, "V")],
    0: [(3, 1, "E1"), (4, 3, "CM"), (4, 3, "K"), (5, 1, "XT", 1), (5, 2, "Q"), (6, 3, "L"), (7, 1, "V")],
    1: [(3, 2, "E1"), (4, 2, "XT", 2), (5, 0, "F1", 0), (5, 1, "F2"), (6, 0, "XT", 3), (6, 2, "Q"), (6, 2, "K"),
        (7, 1, "V")],
    2: [(3, 1, "E1"), (3, 2, "E2"), (4, 0, "E3"), (5, 1, "K"), (6, 0, "XT", 4), (6, 1, "Q"), (6, 3, "V")],
    3: [(3, 1, "E1"), (3, 3, "E2"), (4, 0, "E3"), (4, 3, "XT", 5), (5, 0, "F1", 0), (5, 0, "F1", 1), (5, 3, "F2"),
        (6, 2, "K", 0), (6, 2, "XT", 6), (6, 2, "K", 1), (7, 0, "Q", 0), (7, 0, "Q", 1), (7, 2, "V", 1),
        (8, 0, "V", 0)],
    4: [(3, 3, "E3"), (4, 1, "K"), (5, 3, "XT", 7), (6, 1, "Q"), (7, 1, "V")],
    5: [(3, 0, "E1"), (3, 3, "E2"), (4, 0, "E3")],
}
LATER = {("K", 0): "step", ("K", 1): "step", ("K", 2): "scores", ("K", 3): "scores", ("K", 5): "step",
        ("Q", 0): "scores", ("Q", 1): "step", ("Q", 2): "step", ("Q", 3): "step", ("Q", 5): "step", ("L", 0): "now",
        ("L", 1): "now", ("XT", 0): "now", ("A", 4): "now", ("end", "att", 0): "scores", ("end", "att", 1): "now",
        ("end", "ff", 1): "scores", ("end", "att", 2): "scores", ("end", "att", 3): "now", ("end", "ff", 3): "now",
        ("end", "att", 4): "now", ("end", "att", 5): "scores"}


def make_order():
    extra = {}

    def put(step, slot, *item):
        extra.setdefault((step, slot), []).append(item)

    for s in range(STREAMS):
        for a, pieces in PLAN.items():
            for step, slot, kind, *c in pieces:
                b = a + (kind in ("K", "Q", "V", "L"))
                put(first_unit(a, s) + step, slot, kind, *((s,) if kind in ("CT", "CM") else (c[0], s) if kind == "XT"
                    else (b, s, c[0] if c else 0)))
    out = []
    for n in range(-4, UNITS + 4):
        live = lambda m: 0 <= m < UNITS
        out.append(("STEP", n))
        for part in STEP:
            if isinstance(part, int):
                out += extra.pop((n, part), [])
            elif part == "A":
                out += [("A", n)] * live(n)
            elif part == "S":
                out += [("S", n + 1)] * live(n + 1)
            else:
                out += [(part[0], n - 1, part[1])] * live(n - 1)
    assert not extra, extra
    return out


ORDER = make_order()


def is_norm(it):
    return it[0] == "E1" and it[1] in (0, 1) or it[0] in ("E3", "F2")


def make_dve_pool_order():
    out, waiting = [], {"scores": [], "step": []}
    before_scores = True

    def put(when, item):
        if when == "now" or when == "scores" and not before_scores and item[1] == "rest":
            out.append(item)
        else:
            waiting[when].append(item)

    def flush(when):
        out.extend(waiting[when])
        waiting[when] = []

    for it in ORDER:
        kind = it[0]
        if kind == "STEP":
            flush("scores")
            flush("step")
            before_scores = True
        elif kind == "S":
            out.append((it, "first"))
            flush("scores")
            before_scores = False
        elif is_norm(it):
            for when in ("scores", "step"):
                out += [item for item in waiting[when] if item[1] == "end"]
                waiting[when] = [item for item in waiting[when] if item[1] != "end"]
            out += [(it, "first"), (it, "rest")]
            put(LATER[("end", "ff" if kind == "F2" else "att", it[1])], (it, "end"))
        elif kind in ("K", "Q", "L", "XT", "A"):
            out.append((it, "first"))
            put(LATER.get((kind, unit(it[1])[0] if kind == "A" else it[1]), "now"), (it, "rest"))
        else:
            out.append((it, "first"))
    return out + waiting["scores"] + waiting["step"]


DVE_POOL_ORDER = make_dve_pool_order()
BY_ACT = {"T", "XT", "CT", "CM", "Q", "E2", "F1"}
BY_DVE = {"K", "V", "L", "E1", "E3", "F2"}


def norms():
    out = []
    for it in ORDER:
        if is_norm(it):
            out.append(("ff" if it[0] == "F2" else "att", it[1], it[2]))
    return out


def xb_pieces():
    after = {("ff", 1): "o2", ("att", 2): "o3", ("ff", 3): "o4", ("att", 4): "o5", ("att", 1): "g0", ("att", 3): "g1"}
    return [(after[n[:2]], n[2]) for n in norms() if n[:2] in after], after


INDEX = {
    "tile": [it for it in ORDER if it[0] in BY_ACT | BY_DVE],
    "tile_act": [it for it in ORDER if it[0] in BY_ACT],
    "tile_dve": [it for it in ORDER if it[0] in BY_DVE],
    "unit": [it[1] for it in ORDER if it[0] == "S"],
    "half": [it[1:] for it in ORDER if it[0] == "PV"],
    "ctx": [it[1] for it in ORDER if it[0] == "PV" and it[2] == 1 and (it[1] % 2 == 1 or unit(it[1])[0] == WIDE)],
    "e1": [it[1:] for it in ORDER if it[0] == "E1"],
    "residual": [it[1:3] for it in ORDER if it[0] == "E1" and it[1] in (0, 1)],
    "norm": norms(),
    "xb": xb_pieces()[0],
    "length": [it[1:3] for it in ORDER if it[0] == "L"],
    "mask": [(*it[1:3], c) for it in ORDER if it[0] == "L" for c in range(2)],
    "k_narrow": [it[1:3] for it in ORDER if it[0] == "K" and it[1] != WIDE],
    "q_narrow": [it[1:3] for it in ORDER if it[0] == "Q" and it[1] != WIDE],
    "q0": [it[1:3] for it in ORDER if it[0] == "Q" and it[1] in MASKED_BY_LENGTH],
    "stream": list(range(STREAMS)),
    "wide": [n for n in range(UNITS) if unit(n)[0] == WIDE],
}
COUNT = {k: len(v) for k, v in INDEX.items()}
AT = {k: {key: i for i, key in enumerate(v)} for k, v in INDEX.items()}
XB_AFTER = xb_pieces()[1]


def build(nc, x, ctx_in, mask_ss, mask_bs, weights, col_bias, row_vec, consts, out):
    with ExitStack() as stack:
        def sb(name, shape, dt=F32):
            return stack.enter_context(nc.sbuf_tensor(name, shape, dt))

        def sem(name):
            return stack.enter_context(nc.semaphore(name))

        W = sb("W", [P, W_COLS])
        RV = sb("RV", [P, ROW_COLS])
        CB = sb("CB", [P, CB_COLS])
        ident = sb("ident", [P, P])
        half = sb("half", [P, 1])
        ident_b = sb("ident_b", [P, P], BF16)
        causal_b = sb("causal_b", [P, P], BF16)
        khead = sb("khead", [P, 4])
        qhead = sb("qhead", [P, HU])
        iota = sb("iota", [HU, P])
        ones_b = sb("ones_b", [64, P], BF16)
        mask_ss_b = sb("mask_ss_b", [P, P], BF16)

        per_stream = lambda name, shape, dt=F32: (
            [sb(f"{name}{s}", shape, dt) for s in range(LANES)] * GROUPS)
        per_pair = lambda name, shape, dt=F32: [sb(f"{name}{i}", shape, dt) for i in range(2)]
        x_in, c_in = per_stream("x_in", [P, D]), per_stream("c_in", [P, D])
        X, XB = per_stream("X", [P, D]), per_stream("XB", [P, D])
        XT, CT = per_stream("XT", [P, D]), per_stream("CT", [P, D])
        seen0, seen1 = per_stream("seen0_", [P, 1]), per_stream("seen1_", [P, 1])
        mask_rows_i, mask_rows_b = per_pair("mask_bs_i", [64, P], I32), per_pair("mask_bs_b", [64, P], BF16)
        mask_row = [slice(32 * (s % 2), 32 * (s % 2) + 1) for s in range(STREAMS)]
        mask_bs_i = [mask_rows_i[s % LANES // 2][mask_row[s], :] for s in range(STREAMS)]
        mask_bs_b = [mask_rows_b[s % LANES // 2][mask_row[s], :] for s in range(STREAMS)]

        def wide_and_parts(name, cols, parts):
            offset = nc.sbuf_base
            return sb(name, [P, cols]), [nc.alloc_sbuf_tensor_at(part, [P, n], F32R, offset=offset + 4 * at)[:, :]
                                         for part, at, n in parts]

        QT, KT, Qall, Qhigh, Qlow, Kspread = [], [], [], [], [], []
        for i in range(2):
            q, parts = wide_and_parts(f"QT{i}", 8 * P, [(f"Qhigh{i}_0", 0, D), (f"Qhigh{i}_1", D, D),
                                                        (f"Qlow{i}", 2 * D, D)])
            QT, Qall, Qhigh, Qlow = QT + [q], Qall + [q[:, 3 * D:4 * D]], Qhigh + [parts[0:2]], Qlow + [parts[2]]
            k, parts = wide_and_parts(f"KT{i}", 2 * 8 * P, [(f"Kspread{i}_{u}", u * 8 * P, 8 * P) for u in range(2)])
            KT, Kspread = KT + [k], Kspread + [parts]
        Kall, Kparts = sb("Kall", [P, D]), [sb(f"Kparts{u}", [P, D]) for u in range(2)]
        V16, V64 = per_pair("V16_", [P, HEADS, 32]), per_pair("V64_", [P, HEADS * DK2])
        OT, O, OnT = per_pair("OT", [P, 8 * P]), per_pair("O", [P, D]), per_pair("OnT", [P, D])
        KTp, CmT = [v[:, 0:D] for v in V64], [v[:, D:2 * D] for v in V64]
        LB = [v[0:HU, 2 * D:2 * D + HU * P // 2].bitcast(BF16) for v in V64]
        q0 = per_pair("q0_", [P, 2, HU])
        rsum = per_pair("rsum", [P, HEADS])
        Pr = per_pair("Pr", [P, HU * P])
        PT = per_pair("PT", [P, 4 * P])
        nmax = per_pair("nmax", [P, HU])
        wsum, wrec = per_pair("wsum", [P, HU]), per_pair("wrec", [P, HU])
        stats, mv, rstd, xc = sb("stats", [P, 6]), sb("mv", [P, 2]), per_pair("rstd", [P, 1]), sb("xc", [P, D])
        ne, cnt, crec, lval, lrow = (sb("ne", [HU, 2, P]), sb("cnt", [HU, 2]), sb("crec", [HU, 2]), sb("lval", [HU, 2]),
                                     sb("lrow", [HU, 2, P], BF16))
        absmax = sb("absmax", [P, 1])

        ps = lambda name, n: stack.enter_context(nc.psum_tensor(name, [P, n], F32))
        SC = [ps("SC0", 1024), ps("SC1", 1024)]
        OTp = ps("OTp", 512)
        M = [ps(f"M{i}", 512) for i in range(3)]

        w_in = {name: sem(f"w_{name}") for name, _ in WEIGHTS}
        rows_in, rows_late_in, cols_in, consts_in, masks_in = (sem("rows_in"), sem("rows_late_in"), sem("cols_in"),
                                                               sem("consts_in"), sem("masks_in"))
        m_loaded, mask_done = [sem(f"m_loaded{s}") for s in range(STREAMS)], sem("mask_done")
        x_loaded, c_loaded, stored = ([sem(f"x_loaded{s}") for s in range(STREAMS)],
                                      [sem(f"c_loaded{s}") for s in range(STREAMS)],
                                      [sem(f"stored{s}") for s in range(STREAMS)])
        ready_dve, ready_act = sem("ready_dve"), sem("ready_act")
        cols_scaled = sem("cols_scaled")
        scores = sem("scores")
        context = sem("context")
        tile_full = sem("tile_full")
        tile_act = sem("tile_act")
        tile_dve = sem("tile_dve")
        probs = sem("probs")
        context_out = sem("context_out")
        maxima = sem("maxima")
        q_high, q_low, q_twice = sem("q_high"), sem("q_low"), sem("q_twice")
        k_high, k_low, k_spread0, k_spread1 = (sem("k_high"), sem("k_low"), sem("k_spread0"),
                                               sem("k_spread1"))
        q0_done = sem("q0_done")
        len_cnt, len_rec, len_val, len_row, len_mask = (sem("len_cnt"), sem("len_rec"),
                                                                sem("len_val"), sem("len_row"), sem("len_mask"))
        recip_done, recip_masked = sem("recip_done"), sem("recip_masked")
        summed, stats_done, var_done, eps_done, centred, normed = (
            sem("summed"), sem("stats_done"), sem("var_done"), sem("eps_done"), sem("centred"), sem("normed"))
        rstd_done, xb_half, xb_done = sem("rstd_done"), sem("xb_half"), sem("xb_done")
        abs0, seen0_done, abs1, seen1_done, cm_done = (sem("abs0"), sem("seen0_done"), sem("abs1"), sem("seen1_done"),
                                                       sem("cm_done"))
        wide_sum, wide_rec, wide_norm = sem("wide_sum"), sem("wide_rec"), sem("wide_norm")

        def weight(name, k, a, b):
            n = dict(WEIGHTS)[name]
            return W[:, W_AT[name] + k * n + a:W_AT[name] + k * n + b]

        def row(name, n=D, at=0):
            return RV[:, ROW_AT[name] + at:ROW_AT[name] + at + n]

        from_one = (tile_act, probs, context_out, tile_dve, k_low, k_spread0, k_spread1, len_mask)

        def waiter(eng, r):
            def wait(s, kind, key):
                eng.wait_ge(s, r * COUNT[kind] + (AT[kind][key] + 1 + (s in from_one)))

            def wait_nth(s, kind, i):
                assert s in from_one
                eng.wait_ge(s, r * COUNT[kind] + (max(i + 1, 0) + 1))
            return wait, wait_nth

        def tile_of(it):
            return M[AT["tile"][it] % len(M)]

        def spread(eng, s, u):
            return eng.tensor_tensor(Kspread[s % 2][u].rearrange("p (c e t) -> p c e t", e=4, t=P),
                                     Kparts[u][:, :].rearrange("p (c t) -> p c t", t=P).unsqueeze(2)
                                     .to_broadcast([P, 2, 4, P]),
                                     khead[:, :].unsqueeze(1).unsqueeze(3).to_broadcast([P, 2, 4, P]), ALU.mult)

        def width(a):
            return DK2 if a == WIDE else DK

        block = stack.enter_context(nc.Block())

        @block.sync
        def _(sp):
            def load(r, s):
                sp.dma_start(x_in[s][:, :], x[r * STREAMS + s, :, :]).then_inc(x_loaded[s], 16)
                sp.dma_start(c_in[s][:, :], ctx_in[r * STREAMS + s, :, :]).then_inc(c_loaded[s], 16)
                sp.dma_start(mask_bs_i[s], mask_bs[bass.ds(r * STREAMS + s, 1), :]).then_inc(m_loaded[s], 16)

            def load_weight(name):
                rows, n = W_ROWS.get(name, D), dict(WEIGHTS)[name]
                dst = W[:, W_AT[name]:W_AT[name] + rows // P * n].rearrange("p (k n) -> p k n", n=n)
                sp.dma_start(dst, weights[name].rearrange("(k p) n -> p k n", p=P)).then_inc(w_in[name], 16)

            for s in range(STREAMS - LANES, STREAMS):
                sp.sem_inc(stored[s], 16)
            sp.dma_start(Pr[0][:, 0:C_COLS], consts[:, :]).then_inc(consts_in, 16)
            sp.dma_start(PT[0][:, 0:P].bitcast(I32), mask_ss[:, :]).then_inc(masks_in, 16)
            sp.dma_start(CB[:, :], col_bias[:, :]).then_inc(cols_in, 16)
            load(0, 0)
            for name in ("k0", "q0", "v0"):
                load_weight(name)
            for s in range(1, LANES):
                load(0, s)
            early = ROW_AT[ROWS[ROWS_EARLY][0]]
            sp.dma_start(RV[:, 0:early], row_vec[0:1, 0:early].to_broadcast([P, early])).then_inc(rows_in, 16)
            for name, _n in WEIGHTS[3:8]:
                load_weight(name)
            sp.dma_start(RV[:, early:ROW_COLS],
                         row_vec[0:1, early:ROW_COLS].to_broadcast([P, ROW_COLS - early])).then_inc(rows_late_in, 16)
            for name, _n in WEIGHTS[8:]:
                load_weight(name)

            def store(r, s):
                value = sp.to_reg(r * COUNT["norm"] + (AT["norm"][("att", 5, s)] + 1))
                sp.wait_ge(consts_in, 16)
                sp.wait_ge(normed, value)
                sp.dma_start(out[r * STREAMS + s, :, :], X[s][:, :]).then_inc(stored[s], 16)

            def load_when_free(r, s, before):
                value = sp.to_reg((r if s > before else r - 1) * STREAMS + (before + 1))
                sp.wait_ge(consts_in, 16)
                sp.wait_ge(cm_done, value)
                load(r, s)

            def rest_of_round(r):
                for s in range(LANES, STREAMS):
                    load_when_free(r, s, s - LANES)
                    store(r, s - LANES)

            with sp.Fori(1, ROUNDS) as r:
                rest_of_round(r - 1)
                for s in range(LANES):
                    load_when_free(r, s, STREAMS - LANES + s)
                    store(r - 1, STREAMS - LANES + s)
            rest_of_round(ROUNDS - 1)
            for s in range(STREAMS - LANES, STREAMS):
                store(ROUNDS - 1, s)
            for s in range(STREAMS):
                sp.wait_ge(stored[s], 16 * ROUNDS + (16 if s >= STREAMS - LANES else 0))

        @block.tensor
        def _(pe):
            pe.wait_ge(ready_act, 1)
            pe.wait_ge(ready_dve, 1)
            with pe.Fori(0, ROUNDS) as r:
                wait, wait_nth = waiter(pe, r)

                def free_tile(it):
                    i = AT["tile"][it]
                    if i >= len(M):
                        old = INDEX["tile"][i - len(M)]
                        if old[0] in BY_ACT:
                            wait(tile_act, "tile_act", old)
                        else:
                            wait(tile_dve, "tile_dve", old)
                    else:
                        wait_nth(tile_act, "tile_act", -1)
                        wait_nth(tile_dve, "tile_dve", -1)

                def product(dst, lhsTs, rhss):
                    for k, (a, b) in enumerate(zip(lhsTs, rhss)):
                        last = pe.matmul(dst, a, b, start=(k == 0), stop=(k == len(lhsTs) - 1))
                    return last

                def turn(dst, src, n):
                    for i in range(n):
                        last = pe.transpose(dst[:, i * P:(i + 1) * P], src[:, i * P:(i + 1) * P], ident[:, :])
                    return last

                def by_weight(it, name, src, tiles, first=0):
                    pe.wait_ge(w_in[name], 16)
                    for j in range(tiles):
                        m = (first + j) * P
                        last = product(tile_of(it)[:, j * P:(j + 1) * P],
                                       [weight(name, k, m, m + P) for k in range(KC)],
                                       [src[:, k * P:(k + 1) * P] for k in range(KC)])
                    last.then_inc(tile_full, 1)

                def by_tokens(it, name, src, n, at=0, chunks=KC):
                    pe.wait_ge(w_in[name], 16)
                    product(tile_of(it)[:, 0:n], [src[:, k * P:(k + 1) * P] for k in range(chunks)],
                            [weight(name, k, at, at + n) for k in range(chunks)]).then_inc(tile_full, 1)

                for it in ORDER:
                    kind = it[0]
                    if kind in BY_ACT | BY_DVE:
                        free_tile(it)
                    if kind == "XT":
                        j, s = it[1:]
                        if j == 0:
                            pe.wait_ge(x_loaded[s], r * 16 + 16)
                            src = x_in[s]
                        else:
                            wait(normed, "norm", (*XT_AFTER[j], s))
                            src = X[s]
                        turn(tile_of(it), src, KC).then_inc(tile_full, 1)
                    elif kind == "CT":
                        s = it[1]
                        pe.wait_ge(c_loaded[s], r * 16 + 16)
                        turn(tile_of(it), c_in[s], KC).then_inc(tile_full, 1)
                    elif kind == "CM":
                        s = it[1]
                        wait(cm_done, "stream", s)
                        turn(tile_of(it), O[s % 2], KC).then_inc(tile_full, 1)
                    elif kind in ("K", "V"):
                        _, a, s, c = it
                        if a in (0, 2):
                            wait(tile_act, "tile_act", ("XT", XT_FOR_ATT[a], s))
                            src = XT[s]
                        elif a == 1:
                            wait(tile_act, "tile_act", ("CM", s))
                            src = CmT[s % 2]
                        else:
                            wait(tile_act, "tile_act", ("CT", s))
                            src = CT[s]
                        if kind == "K":
                            by_weight(it, f"k{a}", src, 4 if a == WIDE else 2, 4 * c)
                        else:
                            by_tokens(it, f"v{a}", src, 512 if a == WIDE else D, 512 * c)
                    elif kind == "Q":
                        _, a, s, c = it
                        wait(tile_act, "tile_act", ("XT", XT_FOR_ATT[a], s))
                        by_weight(it, f"q{a}", XT[s], 4 if a == WIDE else 2, 4 * c)
                    elif kind == "L":
                        _, a, s, _c = it
                        wait(q0_done, "q0", (a, s))
                        wait(tile_dve, "tile_dve", ("K", a, s, 0))
                        for c in range(2):
                            last = pe.matmul(tile_of(it)[0:HU, c * P:(c + 1) * P], q0[s % 2][:, c, :],
                                             KTp[s % 2][:, c * P:(c + 1) * P], start=True, stop=True)
                        last.then_inc(tile_full, 1)
                    elif kind == "S":
                        n = it[1]
                        a, s, c = unit(n)
                        wait_nth(probs, "unit", n - 2)
                        q, k, sc = QT[s % 2], KT[s % 2], SC[c]
                        if a == WIDE:
                            wait(tile_act, "tile_act", ("Q", a, s, c))
                            wait(tile_dve, "tile_dve", ("K", a, s, c))
                            for j in range(HU):
                                rows, cols = 64 * (j % 2), (4 * c + j // 2) * P
                                at = (4 * (j % 2) + j // 2) * P
                                last = pe.matmul(sc[:, at:at + P], q[rows:rows + 64, cols:cols + P],
                                                 k[rows:rows + 64, cols:cols + P], start=True, stop=True,
                                                 skip_group_check=True)
                            last.then_inc(scores, 1)
                            continue
                        wait(q_low, "q_narrow", (a, s))
                        wait(q_twice, "q_narrow", (a, s))
                        wait(k_spread0, "k_narrow", (a, s))
                        wait(k_spread1, "k_narrow", (a, s))
                        if a in MASKED_BY_LENGTH:
                            wait(len_mask, "mask", (a, s, c))
                        for u in range(2):
                            rows = slice(64 * u, 64 * u + 64)
                            parts = Kspread[s % 2][u]
                            terms = [(Qhigh[s % 2][u][:, c * P:(c + 1) * P], parts[:, c * 512:(c + 1) * 512]),
                                     (Qlow[s % 2][rows, c * P:(c + 1) * P], parts[rows, c * 512:(c + 1) * 512])]
                            heads = lambda mask: mask.unsqueeze(1).to_broadcast([mask.shape[0], 4, P])
                            if a == 0:
                                terms.append((ident_b[:, :], heads(causal_b[:, :])))
                            if a in MASKED_BY_LENGTH:
                                terms.append((ones_b[0:HU, :], LB[c][:, u * 512:(u + 1) * 512]))
                            if a == 2:
                                terms.append((ident_b[:, :], heads(mask_ss_b[:, :])))
                            if a == 3:
                                wait(mask_done, "stream", s)
                                terms.append((ones_b[mask_row[s], :], heads(mask_bs_b[s])))
                            last = product(sc[:, u * 512:(u + 1) * 512], *zip(*terms))
                        last.then_inc(scores, 1)
                    elif kind == "T":
                        _, n, u = it
                        if unit(n)[0] == WIDE:
                            wait(wide_norm, "wide", n)
                        else:
                            wait(probs, "unit", n)
                        turn(tile_of(it), Pr[n % 2][:, u * 512:(u + 1) * 512], 4).then_inc(tile_full, 1)
                    elif kind == "PV":
                        _, n, u = it
                        a, s, c = unit(n)
                        wait(tile_act, "tile_act", ("T", n, u))
                        if c == 0 and u == 0 or a == WIDE:
                            if n == 0:
                                wait_nth(context_out, "ctx", -1)
                            else:
                                before = [m for m in INDEX["ctx"] if m < n][-1]
                                wait(context_out, "ctx", before)
                        if n % 2 == 0 and u == 0 or a == WIDE:
                            wait(tile_dve, "tile_dve", ("V", a, s, c if a == WIDE else 0))
                        for e in range(4):
                            rhs = PT[u][:, e * P:(e + 1) * P]
                            if a == WIDE:
                                h = HU * c + 2 * e + u
                                last = pe.matmul(OTp[64 * u:64 * u + 64, e * P:(e + 1) * P],
                                                 V64[s % 2][:, h * DK2:(h + 1) * DK2],
                                                 rhs, start=True, stop=True, skip_group_check=True)
                            else:
                                h = HU * c + 4 * u + e
                                cols = (2 * c + u) * P
                                last = pe.matmul(OTp[32 * e:32 * e + 32, cols:cols + P], V16[s % 2][:, h, :], rhs,
                                                 start=True, stop=True, skip_group_check=True)
                        last.then_inc(context, 1)
                    elif kind == "E1":
                        _, a, s, _c = it
                        wait(context_out, "ctx", first_unit(a, s) + 1)
                        turn(tile_of(it), OT[s % 2], 4).then_inc(tile_full, 1)
                    elif kind == "E2":
                        _, a, s, _c = it
                        wait(tile_dve, "tile_dve", ("E1", a, s, 0))
                        turn(tile_of(it), O[s % 2], KC).then_inc(tile_full, 1)
                    elif kind == "E3":
                        _, a, s, _c = it
                        if a == WIDE:
                            wait(context_out, "ctx", first_unit(a, s) + 1)
                            by_tokens(it, f"o{a}", OT[s % 2], D, chunks=HEADS * DK2 // P)
                        else:
                            wait(tile_act, "tile_act", ("E2", a, s, 0))
                            by_tokens(it, f"o{a}", OnT[s % 2], D)
                    elif kind == "F1":
                        _, a, s, c = it
                        wait(tile_act, "tile_act", ("XT", 2 if a == 1 else 5, s))
                        if a == 1:
                            by_weight(it, "f0", XT[s], FF0 // P)
                        else:
                            by_weight(it, "f1", XT[s], 4, 4 * c)
                    elif kind == "F2":
                        _, a, s, _c = it
                        wait(tile_act, "tile_act", ("F1", a, s, 0 if a == 1 else 1))
                        by_tokens(it, "g0" if a == 1 else "g1", QT[s % 2], D, chunks=(FF0 if a == 1 else FF1) // P)

        @block.scalar
        def _(act):
            act.wait_ge(consts_in, 16)
            act.activation(ident[:, :], Pr[0][:, C_AT["ident"]:C_AT["ident"] + P], ACT.Copy)
            act.activation(ident_b[:, :], Pr[0][:, C_AT["ident"]:C_AT["ident"] + P], ACT.Copy)
            act.activation(causal_b[:, :], Pr[0][:, C_AT["causal"]:C_AT["causal"] + P], ACT.Copy).then_inc(ready_act, 1)
            act.sem_inc(tile_act, 1)
            act.sem_inc(probs, 1)
            act.sem_inc(context_out, 1)
            act.wait_ge(ready_dve, 1)
            act.wait_ge(cols_in, 16)
            act.wait_ge(cols_scaled, 1)
            with act.Fori(0, ROUNDS) as r:
                wait, wait_nth = waiter(act, r)
                for it in ORDER:
                    kind = it[0]
                    if kind in BY_ACT:
                        wait(tile_full, "tile", it)
                    if kind == "XT":
                        s = it[2]
                        act.activation(XT[s][:, :], tile_of(it)[:, 0:D], ACT.Copy).then_inc(tile_act, 1)
                    elif kind == "CT":
                        act.activation(CT[it[1]][:, :], tile_of(it)[:, 0:D], ACT.Copy).then_inc(tile_act, 1)
                    elif kind == "CM":
                        act.activation(CmT[it[1] % 2], tile_of(it)[:, 0:D], ACT.Copy).then_inc(tile_act, 1)
                    elif kind == "E2":
                        act.activation(OnT[it[2] % 2][:, :], tile_of(it)[:, 0:D], ACT.Copy).then_inc(tile_act, 1)
                    elif kind == "Q":
                        _, a, s, c = it
                        scale = float(width(a)) ** -0.5
                        if a == WIDE:
                            for j in range(4):
                                b = CB_AT[f"q{a}"] + 4 * c + j
                                last = act.activation(QT[s % 2][:, (4 * c + j) * P:(4 * c + j + 1) * P],
                                                      tile_of(it)[:, j * P:(j + 1) * P], ACT.Identity,
                                                      bias=CB[:, b:b + 1], scale=scale)
                            last.then_inc(tile_act, 1)
                            continue
                        q = Qall[s % 2]
                        if a in (0, 1):
                            last = act.activation(q, tile_of(it)[:, 0:D], ACT.Copy, scale=scale)
                        else:
                            for j in range(2):
                                b = CB_AT[f"q{a}"] + j
                                last = act.activation(q[:, j * P:(j + 1) * P], tile_of(it)[:, j * P:(j + 1) * P],
                                                      ACT.Identity, bias=CB[:, b:b + 1], scale=scale)
                        last.then_inc(tile_act, 1)
                        wait(tile_act, "tile_act", it)
                        for u in range(2):
                            rows = slice(64 * u, 64 * u + 64)
                            last = act.activation(Qhigh[s % 2][u][rows, :], q[rows, :], ACT.Copy)
                        last.then_inc(q_high, 1)
                        for u in range(2):
                            rows, twice = slice(64 * u, 64 * u + 64), slice(64 - 64 * u, P - 64 * u)
                            last = act.activation(Qhigh[s % 2][u][twice, :], q[rows, :], ACT.Copy)
                        last.then_inc(q_twice, 1)
                    elif kind == "F1":
                        _, a, s, c = it
                        for j in range(2 if a == 1 else 4):
                            b = CB_AT["f0" if a == 1 else "f1"] + 4 * c + j
                            last = act.activation(QT[s % 2][:, (4 * c + j) * P:(4 * c + j + 1) * P],
                                                  tile_of(it)[:, j * P:(j + 1) * P], ACT.Relu if a == 1 else ACT.Gelu,
                                                  bias=CB[:, b:b + 1])
                        last.then_inc(tile_act, 1)
                    elif kind == "A":
                        n = it[1]
                        wait(maxima, "unit", n)
                        for h in range(HU):
                            last = act.activation(Pr[n % 2][:, h * P:(h + 1) * P], SC[n % 2][:, h * P:(h + 1) * P],
                                                  ACT.Exp, bias=nmax[n % 2][:, h:h + 1])
                        last.then_inc(probs, 1)
                    elif kind == "T":
                        act.activation(PT[it[2]][:, :], tile_of(it)[:, :], ACT.Copy).then_inc(tile_act, 1)
                    elif kind == "PV" and it[2] == 1 and it[1] in AT["ctx"]:
                        n = it[1]
                        a, s, c = unit(n)
                        wait(context, "half", (n, 1))
                        if a == WIDE:
                            for e in range(4):
                                b = CB_AT[f"v{a}"] + 4 * c + e
                                last = act.activation(OT[s % 2][:, (4 * c + e) * P:(4 * c + e + 1) * P],
                                                      OTp[:, e * P:(e + 1) * P], ACT.Identity, bias=CB[:, b:b + 1])
                        else:
                            last = act.activation(OT[s % 2][:, 0:512], OTp[:, :], ACT.Copy)
                        last.then_inc(context_out, 1)

        @block.vector
        def _(dve):
            dve.wait_ge(consts_in, 16)
            for dst, name, rows, n in ((khead, "khead", P, 4), (qhead, "qhead", P, HU), (iota, "iota", HU, P)):
                dve.tensor_copy(dst[:, :], Pr[0][0:rows, C_AT[name]:C_AT[name] + n])
            dve.wait_ge(ready_act, 1)
            dve.memset(ones_b[:, :], 1.0)
            dve.memset(half[:, :], -0.5)
            dve.wait_ge(masks_in, 16)
            dve.tensor_scalar(mask_ss_b[:, :], PT[0][:, 0:P].bitcast(I32), 0.0, -BIG, ALU.is_equal, ALU.mult)
            for i in range(2):
                dve.memset(V16[i][:, :, DK:DK + 1], 1.0)
                last = dve.memset(V16[i][:, :, DK + 1:32], 0.0)
            last.then_inc(ready_dve, 1)
            dve.sem_inc(tile_dve, 1)
            dve.sem_inc(k_low, 1)
            dve.sem_inc(k_spread0, 1)
            dve.wait_ge(cols_in, 16)
            for name, n in COLUMN_BIASES:
                if name[0] == "q":
                    b = CB[:, CB_AT[name]:CB_AT[name] + n // P]
                    last = dve.tensor_scalar(b, b, float(width(int(name[1]))) ** -0.5, None, ALU.mult)
            last.then_inc(cols_scaled, 1)

            with dve.Fori(0, ROUNDS) as r:
                wait, wait_nth = waiter(dve, r)

                def norm(what, a, s):
                    key, y = (what, a, s), O[s % 2]
                    name = LN_OF[(what, a)]
                    dve.bn_stats(stats[:, :], y[:, :]).then_inc(stats_done, 1)
                    value = dve.to_reg(r * COUNT["norm"] + (AT["norm"][key] + 1))
                    dve.wait_ge(rows_in, 16)
                    dve.wait_ge(stats_done, value)
                    dve.bn_aggr(mv[:, :], stats[:, :]).then_inc(var_done, 1)
                    wait(var_done, "norm", key)
                    i = AT["norm"][key] % 2
                    dve.tensor_scalar(rstd[i][:, :], mv[:, 1:2], EPS, None, ALU.add).then_inc(eps_done, 1)
                    dve.scalar_tensor_tensor(out=xc[:, :], in0=y[:, :], scalar=mv[:, 0:1], in1=row(name + "g"),
                                             op0=ALU.subtract, op1=ALU.mult).then_inc(centred, 1)

                def norm_end(what, a, s):
                    key, i = (what, a, s), AT["norm"][(what, a, s)] % 2
                    name = LN_OF[(what, a)]
                    wait(centred, "norm", key)
                    wait(rstd_done, "norm", key)
                    if (what, a) == ("att", 0):
                        dve.wait_ge(stored[(s - LANES) % STREAMS], r * 16 + 16)
                    dve.scalar_tensor_tensor(out=X[s][:, :], in0=xc[:, :], scalar=rstd[i][:, 0:1],
                                             in1=row(name + "b"), op0=ALU.mult, op1=ALU.add).then_inc(normed, 1)

                def e1_rest(it):
                    _, a, s, _c = it
                    wait(tile_dve, "tile_dve", it)
                    dve.tensor_tensor(O[s % 2][:, :], O[s % 2][:, :], (x_in if a == 0 else X)[s][:, :],
                                      ALU.add).then_inc(summed, 1)
                    wait(summed, "residual", (a, s))
                    norm("att", a, s)

                def mask_context(s):
                    wait(normed, "norm", ("att", 0, s))
                    dve.tensor_reduce(absmax[:, :], X[s][:, :], AX_X, ALU.max,
                                      apply_absolute_value=True).then_inc(abs1, 1)
                    wait(abs1, "stream", s)
                    dve.tensor_scalar(seen1[s][:, :], absmax[:, :], 0.0, None, ALU.is_gt).then_inc(seen1_done, 1)
                    wait(seen1_done, "stream", s)
                    dve.wait_ge(c_loaded[s], r * 16 + 16)
                    dve.tensor_scalar(O[s % 2][:, :], c_in[s][:, :], seen1[s][:, 0:1], None,
                                      ALU.mult).then_inc(cm_done, 1)

                for it, part in DVE_POOL_ORDER:
                    kind = it[0]
                    if kind in BY_DVE and part == "first":
                        wait(tile_full, "tile", it)
                    if part == "end":
                        norm_end("ff" if kind == "F2" else "att", it[1], it[2])
                        if kind == "E1" and it[1] == 0:
                            mask_context(it[2])
                        continue
                    if kind == "XT" and it[1] == 0 and part == "rest":
                        s = it[2]
                        dve.wait_ge(x_loaded[s], r * 16 + 16)
                        dve.tensor_reduce(absmax[:, :], x_in[s][:, :], AX_X, ALU.max,
                                          apply_absolute_value=True).then_inc(abs0, 1)
                        wait(abs0, "stream", s)
                        dve.tensor_scalar(seen0[s][:, :], absmax[:, :], 0.0, None, ALU.is_gt).then_inc(seen0_done, 1)
                        dve.wait_ge(m_loaded[s], r * 16 + 16)
                        dve.tensor_scalar(mask_bs_b[s], mask_bs_i[s], 0.0, -BIG, ALU.is_equal,
                                          ALU.mult).then_inc(mask_done, 1)
                    elif kind == "K" and it[1] == WIDE and part == "first":
                        _, a, s, c = it
                        t = tile_of(it)
                        b = CB_AT[f"k{a}"] + 4 * c
                        last = dve.tensor_tensor(KT[s % 2][:, c * 512:(c + 1) * 512].rearrange("p (j t) -> p j t", t=P),
                                                 t[:, :].rearrange("p (j t) -> p j t", t=P),
                                                 CB[:, b:b + 4].unsqueeze(2).to_broadcast([P, 4, P]), ALU.add)
                        last.then_inc(tile_dve, 1)
                    elif kind == "K" and it[1] != WIDE:
                        _, a, s, c = it
                        t = tile_of(it)
                        k = KTp[s % 2] if a in (0, 1) else Kall[:, :]
                        if part == "first":
                            if a in (0, 1):
                                last = dve.tensor_copy(k, t[:, 0:D])
                            else:
                                wait_nth(k_low, "k_narrow", AT["k_narrow"][(a, s)] - 1)
                                b = CB_AT[f"k{a}"]
                                last = dve.tensor_tensor(k.rearrange("p (j t) -> p j t", t=P),
                                                         t[:, 0:D].rearrange("p (j t) -> p j t", t=P),
                                                         CB[:, b:b + 2].unsqueeze(2).to_broadcast([P, 2, P]), ALU.add)
                            last.then_inc(tile_dve, 1)
                            continue
                        wait(tile_dve, "tile_dve", it)
                        for spread_done in (k_spread0, k_spread1):
                            wait_nth(spread_done, "k_narrow", AT["k_narrow"][(a, s)] - 1)
                        own, other = (slice(0, 64), slice(64, P)), (slice(64, P), slice(0, 64))
                        for u in range(2):
                            last = dve.tensor_copy(Kparts[u][own[u], :].bitcast(F32R), k[own[u], :])
                        last.then_inc(k_high, 1)
                        wait(k_high, "k_narrow", (a, s))
                        for u in range(2):
                            last = dve.tensor_tensor(Kparts[u][other[u], :].bitcast(F32R), k[own[u], :],
                                                     Kparts[u][own[u], :], ALU.subtract)
                        last.then_inc(k_low, 1)
                        wait(k_low, "k_narrow", (a, s))
                        spread(dve, s, 0).then_inc(k_spread0, 1)
                    elif kind == "Q" and it[1] in MASKED_BY_LENGTH and part == "first":
                        _, a, s, c = it
                        wait(tile_act, "tile_act", it)
                        first = Qall[s % 2].rearrange("p (c t) -> p c t", t=P)[:, :, 0:1]
                        dve.tensor_tensor(q0[s % 2][:, :, :], first.to_broadcast([P, 2, HU]),
                                          qhead[:, :].unsqueeze(1).to_broadcast([P, 2, HU]),
                                          ALU.mult).then_inc(q0_done, 1)
                    elif kind == "Q" and it[1] != WIDE and part == "rest":
                        _, a, s, c = it
                        wait(q_high, "q_narrow", (a, s))
                        for u in range(2):
                            rows = slice(64 * u, 64 * u + 64)
                            last = dve.tensor_tensor(Qlow[s % 2][rows, :], Qall[s % 2][rows, :],
                                                     Qhigh[s % 2][u][rows, :].bitcast(F32), ALU.subtract)
                        last.then_inc(q_low, 1)
                    elif kind == "V" and part == "first":
                        _, a, s, c = it
                        if a == WIDE:
                            last = dve.tensor_copy(V64[s % 2][:, 512 * c:512 * (c + 1)], tile_of(it)[:, :])
                        else:
                            src = tile_of(it)[:, 0:D].rearrange("p (h d) -> p h d", d=DK)
                            dst = V16[s % 2][:, :, 0:DK]
                            if a in (0, 1):
                                last = dve.tensor_copy(dst, src)
                            else:
                                if a == 2 and s == 0:
                                    dve.wait_ge(rows_late_in, 16)
                                last = dve.tensor_tensor(dst, src, row(f"v{a}").rearrange("p (h d) -> p h d", d=DK),
                                                         ALU.add)
                        last.then_inc(tile_dve, 1)
                    elif kind == "L":
                        _, a, s, _c = it
                        key = (a, s)
                        if part == "first":
                            dve.tensor_scalar(ne[:, :, :], tile_of(it)[0:HU, 0:2 * P].rearrange("p (c t) -> p c t", t=P),
                                              0.0, None, ALU.not_equal).then_inc(tile_dve, 1)
                            continue
                        wait(tile_dve, "tile_dve", it)
                        dve.tensor_reduce(cnt[:, :], ne[:, :, :], AX_X, ALU.add).then_inc(len_cnt, 1)
                        wait(len_cnt, "length", key)
                        dve.reciprocal(crec[:, :], cnt[:, :]).then_inc(len_rec, 1)
                        wait(len_rec, "length", key)
                        dve.scalar_tensor_tensor(out=lval[:, :], in0=crec[:, :], scalar=-BIG, in1=cnt[:, :],
                                                 op0=ALU.mult, op1=ALU.mult).then_inc(len_val, 1)
                        wait(len_val, "length", key)
                        wait_nth(len_mask, "mask", AT["mask"][(a, s, 0)] - 1)
                        for c in range(2):
                            last = dve.tensor_scalar(lrow[:, c, :], iota[:, :], cnt[:, c:c + 1], lval[:, c:c + 1],
                                                     ALU.is_ge, ALU.mult)
                        last.then_inc(len_row, 1)
                    elif kind == "S":
                        n = it[1]
                        wait(scores, "unit", n)
                        i = n % 2
                        dve.tensor_reduce(nmax[i][:, :], SC[i][:, :].rearrange("p (h t) -> p h t", t=P), AX_X, ALU.max,
                                          negate=True).then_inc(maxima, 1)
                    elif kind == "A" and unit(it[1])[0] == WIDE and part == "rest":
                        n = it[1]
                        i = n % 2
                        wait(probs, "unit", n)
                        dve.tensor_reduce(wsum[i][:, :], Pr[i][:, :].rearrange("p (h t) -> p h t", t=P), AX_X,
                                          ALU.add).then_inc(wide_sum, 1)
                        wait(wide_sum, "wide", n)
                        dve.reciprocal(wrec[i][:, :], wsum[i][:, :]).then_inc(wide_rec, 1)
                    elif kind == "E1":
                        _, a, s, _c = it
                        t = tile_of(it)[:, :].rearrange("p (h d) -> p h d", d=32)
                        rec = rsum[s % 2]
                        key = (a, s, 0)
                        if part == "rest":
                            if a in (0, 1):
                                e1_rest(it)
                            continue
                        dve.reciprocal(rec[:, :].unsqueeze(2), t[:, :, DK:DK + 1]).then_inc(recip_done, 1)
                        wait(recip_done, "e1", key)
                        if a in (0, 1):
                            if a == 0:
                                wait(seen0_done, "stream", s)
                            else:
                                wait(seen1_done, "stream", s)
                            dve.tensor_scalar(rec[:, :], rec[:, :], (seen0, seen1)[a][s][:, 0:1], None,
                                              ALU.mult).then_inc(recip_masked, 1)
                            wait(recip_masked, "residual", (a, s))
                        dve.tensor_tensor(O[s % 2][:, :].rearrange("p (h d) -> p h d", d=DK), t[:, :, 0:DK],
                                          rec[:, :].unsqueeze(2).to_broadcast([P, HEADS, DK]), ALU.mult)\
                           .then_inc(tile_dve, 1)
                    elif kind == "E3":
                        _, a, s, _c = it
                        if part == "rest":
                            wait(tile_dve, "tile_dve", it)
                            norm("att", a, s)
                            continue
                        wait(xb_done, "xb", (f"o{a}", s))
                        dve.tensor_tensor(O[s % 2][:, :], tile_of(it)[:, 0:D], XB[s][:, :], ALU.add).then_inc(tile_dve, 1)
                    elif kind == "F2":
                        _, a, s, _c = it
                        if part == "rest":
                            wait(tile_dve, "tile_dve", it)
                            norm("ff", a, s)
                            continue
                        wait(xb_done, "xb", ("g0" if a == 1 else "g1", s))
                        if a == 1:
                            dve.scalar_tensor_tensor(out=O[s % 2][:, :], in0=tile_of(it)[:, 0:D], scalar=seen0[s][:, 0:1],
                                                     in1=XB[s][:, :], op0=ALU.mult, op1=ALU.add).then_inc(tile_dve, 1)
                        else:
                            dve.tensor_tensor(O[s % 2][:, :], tile_of(it)[:, 0:D], XB[s][:, :],
                                              ALU.add).then_inc(tile_dve, 1)

        @block.gpsimd
        def _(pool):
            pool.wait_ge(ready_dve, 1)
            pool.sem_inc(k_spread1, 1)
            pool.sem_inc(len_mask, 1)
            with pool.Fori(0, ROUNDS) as r:
                wait, wait_nth = waiter(pool, r)

                def invert_deviation(what, a, s):
                    key = (what, a, s)
                    i = AT["norm"][key] % 2
                    wait(eps_done, "norm", key)
                    pool.tensor_tensor(rstd[i][:, :], rstd[i][:, :], half[:, :], ALU.pow).then_inc(rstd_done, 1)

                def add_bias(what, a, s):
                    key = (what, a, s)
                    if (what, a) not in XB_AFTER:
                        return
                    name = XB_AFTER[(what, a)]
                    wait(normed, "norm", key)
                    pool.wait_ge(rows_in, 16)
                    if name == "g0":
                        pool.tensor_tensor(XB[s][:, :], row("g0"), seen0[s][:, 0:1].to_broadcast([P, D]),
                                           ALU.mult).then_inc(xb_half, 1)
                        wait(xb_half, "stream", s)
                        pool.tensor_tensor(XB[s][:, :], XB[s][:, :], X[s][:, :], ALU.add).then_inc(xb_done, 1)
                    else:
                        if name == "o2" and s == 0:
                            pool.wait_ge(rows_late_in, 16)
                        pool.tensor_tensor(XB[s][:, :], X[s][:, :], row(name), ALU.add).then_inc(xb_done, 1)

                for it, part in DVE_POOL_ORDER:
                    kind = it[0]
                    if part == "first":
                        continue
                    if kind == "A" and unit(it[1])[0] == WIDE:
                        n = it[1]
                        i = n % 2
                        wait(wide_rec, "wide", n)
                        p = Pr[i][:, :].rearrange("p (h t) -> p h t", t=P)
                        pool.tensor_tensor(p, p, wrec[i][:, :].unsqueeze(2).to_broadcast([P, HU, P]),
                                           ALU.mult).then_inc(wide_norm, 1)
                    elif kind == "K" and it[1] != WIDE:
                        _, a, s, c = it
                        wait(k_low, "k_narrow", (a, s))
                        spread(pool, s, 1).then_inc(k_spread1, 1)
                    elif kind == "L":
                        _, a, s, _c = it
                        wait(len_row, "length", (a, s))
                        for c in range(2):
                            pool.tensor_tensor(LB[c].rearrange("p (h t) -> p h t", t=P),
                                               ident[0:HU, 0:HU].unsqueeze(2).to_broadcast([HU, HU, P]),
                                               lrow[:, c:c + 1, :].to_broadcast([HU, HU, P]),
                                               ALU.mult).then_inc(len_mask, 1)
                    elif is_norm(it):
                        what = "ff" if kind == "F2" else "att"
                        (invert_deviation if part == "rest" else add_bias)(what, it[1], it[2])


def shape_constants():
    c = np.zeros((P, C_COLS), np.float32)
    p = np.arange(P)[:, None]
    t = np.arange(P)[None, :]
    c[:, C_AT["ident"]:][:, :P] = p == t
    c[:, C_AT["causal"]:][:, :P] = np.where(t > p, -BIG, 0.0)
    c[:, C_AT["khead"]:][:, :4] = p % 64 // DK == np.arange(4)[None, :]
    c[:, C_AT["qhead"]:][:, :HU] = p // DK == np.arange(HU)[None, :]
    c[:, C_AT["iota"]:][:, :P] = t
    return c


def kernel(**inputs):
    import concourse.bacc as bacc
    from concourse.bass_utils import run_bass_kernel_spmd as run

    v = {k: np.asarray(a) for k, a in inputs.items()}
    heads_last = lambda w: np.ascontiguousarray(np.transpose(w, (1, 0, 2)).reshape(D, -1))
    L0, L1, L2, L3 = "L0_xattn_", "L1_xattn_", "L2_xattn_", "L3_xattn_"
    qkv = v[L3 + "W_qkv"]
    w = {
        "q0": heads_last(v[L0 + "Wq1"]), "k0": heads_last(v[L0 + "Wk1"]), "v0": heads_last(v[L0 + "Wv1"]),
        "q1": heads_last(v[L0 + "Wq2"]), "k1": heads_last(v[L0 + "Wk2"]), "v1": heads_last(v[L0 + "Wv2"]),
        "f0": v[L0 + "fc1_w"].T, "g0": v[L0 + "fc2_w"].T,
        "q2": v[L1 + "self_wq"], "k2": v[L1 + "self_wk"], "v2": v[L1 + "self_wv"], "o2": v[L1 + "self_wo"],
        "q3": v[L1 + "cross_wq"], "k3": v[L1 + "cross_wk"], "v3": v[L1 + "cross_wv"], "o3": v[L1 + "cross_wo"],
        "f1": v[L1 + "ff_w1"], "g1": v[L1 + "ff_w2"],
        "q4": v[L2 + "Wq"], "k4": v[L2 + "Wk"], "v4": v[L2 + "Wv"], "o4": v[L2 + "Wo"],
        "q5": qkv[:D].T, "k5": qkv[D:2 * D].T, "v5": qkv[2 * D:].T, "o5": v[L3 + "W_o"].T,
    }
    b3 = v[L3 + "b_qkv"]
    cb = {"f0": v[L0 + "fc1_b"], "q2": v[L1 + "self_bq"], "k2": v[L1 + "self_bk"], "q3": v[L1 + "cross_bq"],
          "k3": v[L1 + "cross_bk"], "f1": v[L1 + "ff_b1"], "q4": v[L2 + "bq"], "k4": v[L2 + "bk"], "v4": v[L2 + "bv"],
          "q5": b3[:D], "k5": b3[D:2 * D]}
    rows = {"ln0g": v[L0 + "ln1_g"], "ln0b": v[L0 + "ln1_b"], "ln1g": v[L0 + "ln2_g"], "ln1b": v[L0 + "ln2_b"],
            "lnfg": v[L0 + "ln3_g"], "lnfb": v[L0 + "ln3_b"], "g0": v[L0 + "fc2_b"], "v2": v[L1 + "self_bv"],
            "o2": v[L1 + "self_bo"], "ln2g": v[L1 + "n1_g"], "ln2b": v[L1 + "n1_b"], "v3": v[L1 + "cross_bv"],
            "o3": v[L1 + "cross_bo"], "ln3g": v[L1 + "n2_g"], "ln3b": v[L1 + "n2_b"], "g1": v[L1 + "ff_b2"],
            "lnhg": v[L1 + "n3_g"], "lnhb": v[L1 + "n3_b"], "o4": v[L2 + "bo"],
            "ln4g": v[L2 + "gamma"], "ln4b": v[L2 + "beta"], "v5": b3[2 * D:], "o5": v[L3 + "b_o"],
            "ln5g": v[L3 + "ln_gamma"], "ln5b": v[L3 + "ln_beta"]}
    arrays = {f"w_{name}": np.ascontiguousarray(w[name]) for name, _ in WEIGHTS}
    arrays["col_bias"] = np.ascontiguousarray(
        np.concatenate([cb[name].reshape(-1, P).T for name, _ in COLUMN_BIASES], axis=1))
    arrays["row_vec"] = np.ascontiguousarray(np.concatenate([rows[name] for name, _ in ROWS])[None, :])
    arrays["consts"] = shape_constants()
    arrays["x"] = np.ascontiguousarray(v["x"])
    arrays["ctx_in"] = np.ascontiguousarray(v["ctx_1024"])
    arrays["mask_ss"] = np.ascontiguousarray(v["mask_SxS2_ik0"])
    arrays["mask_bs"] = np.ascontiguousarray(v["mask_Bx1x1xS2_if1"].reshape(BATCH, SEQ))

    nc = bacc.Bacc("TRN2", target_bir_lowering=False, num_devices=1)
    ap = {k: nc.dram_tensor(k, a.shape, mybir.dt.from_np(a.dtype), kind="ExternalInput").ap() for k, a in arrays.items()}
    out = nc.dram_tensor("out", (BATCH, SEQ, D), F32, kind="ExternalOutput").ap()
    build(nc, ap["x"], ap["ctx_in"], ap["mask_ss"], ap["mask_bs"], {name: ap[f"w_{name}"] for name, _ in WEIGHTS},
          ap["col_bias"], ap["row_vec"], ap["consts"], out)
    r = run(nc, [arrays], core_ids=[0])
    return r.results[0]["out"]
```
